# Optimizing a Trainium2 kernel written in Bass

```python
import numpy as np
import jax
import jax.numpy as jnp

def _softmax(x, axis=-1):
    return jax.nn.softmax(x, axis=axis)

def _gelu(x):
    return jax.nn.gelu(x, approximate=True)

def _silu(x):
    return jax.nn.silu(x)

def _sigmoid(x):
    return jax.nn.sigmoid(x)

def _layernorm(x, axis=-1, eps=1e-05):
    m = jnp.mean(x, axis=axis, keepdims=True)
    v = jnp.var(x, axis=axis, keepdims=True)
    return (x - m) / jnp.sqrt(v + eps)

def _scatter_add(tgt, idx, src, axis=0):
    return tgt.at[idx].add(src)

def _segment_sum(src, seg, n):
    return jax.ops.segment_sum(src, seg, n)
kernel_name = 'mk_macaron_d1_jaxref_r4_fb561a'

def setup_inputs(seed: int=0):
    np.random.seed(seed)
    _w = jnp.asarray

    def _L0_attn_setup():
        import jax, jax.numpy as jnp
        import numpy as np
        HEADS = 16
        key = jax.random.key(seed)
        k1, k2, k3 = jax.random.split(key, 3)
        B, N, C = (4, 1024, 256)
        x = jax.random.normal(k1, (B, N, C), dtype=jnp.float32)
        w_qkv = jax.random.normal(k2, (3 * C, C), dtype=jnp.float32) * C ** (-0.5)
        w_proj = jax.random.normal(k3, (C, C), dtype=jnp.float32) * C ** (-0.5)
        b_proj = jnp.zeros((C,), dtype=jnp.float32)
        return {'x': x, 'w_qkv': w_qkv, 'w_proj': w_proj, 'b_proj': b_proj}
    _L0_attn_in = _L0_attn_setup()

    def _L0_ffn_setup():
        import jax, jax.numpy as jnp
        import numpy as np
        DIM = 256
        E = 16
        TOPK = 2
        G = 4
        TOPK_G = 2
        INTER = 128
        N_SHARED = 2
        ROUTE_SCALE = 1.0

        def _gate(xf, gate_w, gate_b):
            scores = xf @ gate_w.T
            scores = jax.nn.softmax(scores.astype(jnp.float32), axis=-1)
            orig = scores
            scores = scores + gate_b
            T = xf.shape[0]
            sg = scores.reshape(T, G, E // G)
            group_scores = jax.lax.top_k(sg, 2)[0].sum(-1)
            _, gidx = jax.lax.top_k(group_scores, TOPK_G)
            keep = jax.nn.one_hot(gidx, G).sum(axis=1) > 0
            sg = jnp.where(keep[:, :, None], sg, -jnp.inf)
            scores = sg.reshape(T, E)
            _, idx = jax.lax.top_k(scores, TOPK)
            weights = jnp.take_along_axis(orig, idx, axis=1)
            weights = (weights * ROUTE_SCALE).astype(xf.dtype)
            return (weights, idx)
        key = jax.random.key(seed)
        ks = jax.random.split(key, 16)
        s = lambda fan_in: 1.0 / np.sqrt(fan_in)
        inp = {'x': jax.random.normal(ks[0], (4, 256, DIM), dtype=jnp.float32), 'gate_w': jax.random.normal(ks[1], (E, DIM), dtype=jnp.float32) * s(DIM), 'gate_b': jnp.zeros((E,), dtype=jnp.float32), 'We1': jax.random.normal(ks[2], (E, DIM, INTER), dtype=jnp.float32) * s(DIM), 'be1': jnp.zeros((E, INTER), dtype=jnp.float32), 'We2': jax.random.normal(ks[3], (E, INTER, DIM), dtype=jnp.float32) * s(INTER), 'be2': jnp.zeros((E, DIM), dtype=jnp.float32), 'We3': jax.random.normal(ks[4], (E, DIM, INTER), dtype=jnp.float32) * s(DIM), 'be3': jnp.zeros((E, INTER), dtype=jnp.float32), 'ws1': jax.random.normal(ks[5], (DIM, N_SHARED * INTER), dtype=jnp.float32) * s(DIM), 'bs1': jnp.zeros((N_SHARED * INTER,), dtype=jnp.float32), 'ws2': jax.random.normal(ks[6], (N_SHARED * INTER, DIM), dtype=jnp.float32) * s(N_SHARED * INTER), 'bs2': jnp.zeros((DIM,), dtype=jnp.float32), 'ws3': jax.random.normal(ks[7], (DIM, N_SHARED * INTER), dtype=jnp.float32) * s(DIM), 'bs3': jnp.zeros((N_SHARED * INTER,), dtype=jnp.float32)}
        return inp
    _L0_ffn_in = _L0_ffn_setup()
    _d = {'L0_attn_x': _L0_attn_in['x'], 'L0_attn_w_qkv': _L0_attn_in['w_qkv'], 'L0_attn_w_proj': _L0_attn_in['w_proj'], 'L0_attn_b_proj': _L0_attn_in['b_proj'], 'L0_ffn_gate_w': _L0_ffn_in['gate_w'], 'L0_ffn_gate_b': _L0_ffn_in['gate_b'], 'L0_ffn_We1': _L0_ffn_in['We1'], 'L0_ffn_be1': _L0_ffn_in['be1'], 'L0_ffn_We2': _L0_ffn_in['We2'], 'L0_ffn_be2': _L0_ffn_in['be2'], 'L0_ffn_We3': _L0_ffn_in['We3'], 'L0_ffn_be3': _L0_ffn_in['be3'], 'L0_ffn_ws1': _L0_ffn_in['ws1'], 'L0_ffn_bs1': _L0_ffn_in['bs1'], 'L0_ffn_ws2': _L0_ffn_in['ws2'], 'L0_ffn_bs2': _L0_ffn_in['bs2'], 'L0_ffn_ws3': _L0_ffn_in['ws3'], 'L0_ffn_bs3': _L0_ffn_in['bs3']}
    _x0 = _d['L0_attn_x']
    _d['L0_attn_x'] = jax.random.normal(jax.random.fold_in(jax.random.key(seed), 1), (8, 1024, 256), dtype=_x0.dtype)
    del _x0
    return _d

def reference(L0_attn_x, L0_attn_w_qkv, L0_attn_w_proj, L0_attn_b_proj, L0_ffn_gate_w, L0_ffn_gate_b, L0_ffn_We1, L0_ffn_be1, L0_ffn_We2, L0_ffn_be2, L0_ffn_We3, L0_ffn_be3, L0_ffn_ws1, L0_ffn_bs1, L0_ffn_ws2, L0_ffn_bs2, L0_ffn_ws3, L0_ffn_bs3):

    def _L0_attn_ref(x, w_qkv, w_proj, b_proj):
        import jax, jax.numpy as jnp
        import numpy as np
        HEADS = 16
        B, N, C = x.shape
        H = HEADS
        D = C // H
        qkv = x @ w_qkv.T
        q, k, v = jnp.split(qkv, 3, axis=-1)

        def to_bhdn(t):
            return t.reshape(B, N, H, D).transpose(0, 2, 3, 1)
        q = jax.nn.relu(to_bhdn(q))
        k = jax.nn.relu(to_bhdn(k))
        v = to_bhdn(v)
        eps = jnp.finfo(q.dtype).eps
        ksum = k.sum(axis=-1)
        z = 1.0 / (jnp.einsum('bhd,bhdn->bhn', ksum, q) + eps)
        context = jnp.einsum('bhdn,bhen->bhde', v, k)
        out = jnp.einsum('bhde,bhen->bhdn', context, q)
        out = out * z[:, :, None, :]
        out = out.transpose(0, 3, 1, 2).reshape(B, N, C)
        return out @ w_proj.T + b_proj

    def _L0_ffn_ref(x, gate_w, gate_b, We1, be1, We2, be2, We3, be3, ws1, bs1, ws2, bs2, ws3, bs3):
        import jax, jax.numpy as jnp
        import numpy as np
        DIM = 256
        E = 16
        TOPK = 2
        G = 4
        TOPK_G = 2
        INTER = 128
        N_SHARED = 2
        ROUTE_SCALE = 1.0

        def _gate(xf, gate_w, gate_b):
            scores = xf @ gate_w.T
            scores = jax.nn.softmax(scores.astype(jnp.float32), axis=-1)
            orig = scores
            scores = scores + gate_b
            T = xf.shape[0]
            sg = scores.reshape(T, G, E // G)
            group_scores = jax.lax.top_k(sg, 2)[0].sum(-1)
            _, gidx = jax.lax.top_k(group_scores, TOPK_G)
            keep = jax.nn.one_hot(gidx, G).sum(axis=1) > 0
            sg = jnp.where(keep[:, :, None], sg, -jnp.inf)
            scores = sg.reshape(T, E)
            _, idx = jax.lax.top_k(scores, TOPK)
            weights = jnp.take_along_axis(orig, idx, axis=1)
            weights = (weights * ROUTE_SCALE).astype(xf.dtype)
            return (weights, idx)
        shape = x.shape
        xf = x.reshape(-1, DIM)
        weights, idx = _gate(xf, gate_w, gate_b)
        combine = (jax.nn.one_hot(idx, E, dtype=xf.dtype) * weights[..., None]).sum(1)
        h1 = jnp.einsum('td,edi->tei', xf, We1) + be1
        h3 = jnp.einsum('td,edi->tei', xf, We3) + be3
        h = jax.nn.silu(h1) * h3
        yo = jnp.einsum('tei,eid->ted', h, We2) + be2
        y = jnp.einsum('te,ted->td', combine, yo)
        z = jax.nn.silu(xf @ ws1 + bs1) * (xf @ ws3 + bs3) @ ws2 + bs2
        return (y + z).reshape(shape)
    x = L0_attn_x
    x = x + 0.5 * _L0_ffn_ref(_layernorm(x, axis=-1), L0_ffn_gate_w, L0_ffn_gate_b, L0_ffn_We1, L0_ffn_be1, L0_ffn_We2, L0_ffn_be2, L0_ffn_We3, L0_ffn_be3, L0_ffn_ws1, L0_ffn_bs1, L0_ffn_ws2, L0_ffn_bs2, L0_ffn_ws3, L0_ffn_bs3)
    x = x + _L0_attn_ref(_layernorm(x, axis=-1), L0_attn_w_qkv, L0_attn_w_proj, L0_attn_b_proj)
    x = x + 0.5 * _L0_ffn_ref(_layernorm(x, axis=-1), L0_ffn_gate_w, L0_ffn_gate_b, L0_ffn_We1, L0_ffn_be1, L0_ffn_We2, L0_ffn_be2, L0_ffn_We3, L0_ffn_be3, L0_ffn_ws1, L0_ffn_bs1, L0_ffn_ws2, L0_ffn_bs2, L0_ffn_ws3, L0_ffn_bs3)
    return x

_drawn_inputs = setup_inputs


def setup_inputs(seed=0):
    import zlib

    import numpy as np

    out = dict(_drawn_inputs(seed))
    spreads = {'L0_attn_b_proj': (0.0, 0.1),
     'L0_ffn_gate_b': (0.0, 0.1),
     'L0_ffn_be1': (0.0, 0.556),
     'L0_ffn_be2': (0.0, 0.343),
     'L0_ffn_be3': (0.0, 0.547),
     'L0_ffn_bs1': (0.0, 0.1),
     'L0_ffn_bs2': (0.0, 0.1),
     'L0_ffn_bs3': (0.0, 0.1)}
    factors = {}
    for name, (base, spread) in spreads.items():
        noise = np.random.default_rng([zlib.crc32(name.encode()), seed]).standard_normal(out[name].shape)
        drawn = base * np.exp(spread * noise) if base else spread * noise
        out[name] = jnp.asarray(drawn.astype(out[name].dtype))
    for name, factor in factors.items():
        out[name] = (out[name] * factor).astype(out[name].dtype)
    return out
```

```python
from contextlib import ExitStack

import numpy as np

import concourse.bass as bass
from concourse import mybir

FP32, BF16 = mybir.dt.float32, mybir.dt.bfloat16
I32, U32 = mybir.dt.int32, mybir.dt.uint32
ALU, ACT, AX = mybir.AluOpType, mybir.ActivationFunctionType, mybir.AxisListType

P = 128
BATCHES, SEQ, C = 8, 1024, 256
TOKENS = BATCHES * SEQ
NT = SEQ // P
KC = C // P
E, GROUPS, INTER = 16, 4, 128
PER_GROUP = E // GROUPS
SHARED = 2 * INTER
HALF = SEQ // 2
HEADS, HD = 16, 16
CH = P // HD
LN_EPS = 1e-5
EPS = float(np.finfo(np.float32).eps)

ROW = C + 5
REGION = TOKENS + P
TILES = 2 * TOKENS // P + E
SPARE = E * REGION
SPARE_TILES = TILES - 2 * TOKENS // P
XG_ROWS = SPARE + SPARE_TILES * P
TQ = P * 2

BE13, BE2 = 0, E * 2 * INTER
BS2 = BE2 + E * C
BPROJ = BS2 + C
NBIAS = BPROJ + C

SLOTS = 8
LOOPED = (8, 136)


class Names:
    pass


class At:

    def __init__(self, k, q=0, n=4):
        self.k, self.q, self.n = k, q, n

    def __add__(self, d):
        return At(self.k + d, self.q, self.n)

    def times(self, m, d=0):
        if isinstance(self.q, int):
            return m * (self.n * self.q + self.k) + d
        return self.q * (m * self.n) + (m * self.k + d)

    def slot(self, n):
        return self.k % n

    def turn(self, n, m, d=0):
        if isinstance(self.q, int):
            return m * ((self.n * self.q + self.k) // n) + d
        return self.q * (m * (self.n // n)) + (m * (self.k // n) + d)


def wait(eng, sem, count):
    if not isinstance(count, int) or count > 0:
        eng.wait_ge(sem, count)


def apart(eng, passed):
    eng.sem_inc(passed, 1)


class Chain:

    def __init__(self, eng, sem, base=0, passed=None):
        self.eng, self.sem, self.base, self.n, self.passed = eng, sem, base, 0, passed

    def did(self, ins):
        self.n += 1
        ins.then_inc(self.sem, 1)

    def settle(self):
        self.eng.wait_ge(self.sem, self.base + self.n)
        if self.passed is not None:
            apart(self.eng, self.passed)

    def then(self, ins):
        self.did(ins)
        self.settle()


def allocate(nc, ctx):
    m = Names()

    def sb(name, shape, dt=FP32):
        return ctx.enter_context(nc.sbuf_tensor(name, shape, dt))

    m.xres = sb("xres", [P, BATCHES, NT, C])
    m.w13 = sb("w13", [P, E * KC * 2 * INTER])
    m.w2 = sb("w2", [P, E * C])
    m.bias_rows = sb("bias_rows", [P, NBIAS], BF16)
    m.gate_w = sb("gate_w", [P, KC, E])
    m.gate_b = sb("gate_b", [P, E])
    m.ws1 = sb("ws1", [P, KC, SHARED])
    m.ws3 = sb("ws3", [P, KC, SHARED])
    m.ws2 = sb("ws2", [P, KC, C])
    m.bs1 = sb("bs1", [P, KC])
    m.bs3 = sb("bs3", [P, KC])
    m.w_qkv = sb("w_qkv", [P, KC, 3 * C])
    m.w_proj = sb("w_proj", [P, KC, C])
    m.ident = sb("ident", [P, P])
    m.ones3 = sb("ones3", [P, P], BF16)
    m.ones_b = sb("ones_b", [P, P], BF16)
    m.before = sb("before", [P, P], BF16)
    m.rev = sb("rev", [P, E])
    m.earlier = sb("earlier", [P, GROUPS, GROUPS])
    m.region0 = sb("region0", [P, E])
    m.part = sb("part", [P, 1])
    m.tile_no = sb("tile_no", [P, 2])
    m.head_mask = sb("head_mask", [P, P])
    m.head_of = sb("head_of", [P, CH])
    m.minus_half = sb("minus_half", [P, NT])
    m.pad = sb("pad", [P, ROW])
    m.rows = sb("rows", [P, 2 * NT * ROW])
    m.xnT = sb("xnT", [P, KC, SEQ])
    m.work = sb("work", [P, 4 * HALF])
    m.stat = sb("stat", [P, NT, 6])
    m.mv = sb("mv", [P, NT, 2])
    m.ve = sb("ve", [P, NT])
    m.rstd = sb("rstd", [P, NT])
    m.mr = sb("mr", [P, NT])
    m.nmr = sb("nmr", [P, NT])
    m.mx = sb("mx", [P, NT])
    m.sm = sb("sm", [P, NT])
    m.rs = sb("rs", [P, NT])
    m.m1 = sb("m1", [P, NT])
    m.rr = sb("rr", [P, 2, NT])
    m.m2 = sb("m2", [P, NT])
    m.tok = sb("tok", [P, NT])
    m.sh = sb("sh", [P, NT, E])
    m.ex = sb("ex", [P, NT, E])
    m.pr = sb("pr", [P, NT, E])
    m.sc = sb("sc", [P, NT, E])
    m.ms = sb("ms", [P, NT, E])
    m.e1 = sb("e1", [P, NT, E])
    m.ms2 = sb("ms2", [P, NT, E])
    m.pos = sb("pos", [P, NT, E])
    m.chosen = sb("chosen", [P, 2, NT, E])
    m.prod = sb("prod", [P, 2, NT, E])
    m.hi = sb("hi", [P, NT * GROUPS, 2])
    m.lo = sb("lo", [P, NT * GROUPS, 2])
    m.t1 = sb("t1", [P, NT * GROUPS, 1])
    m.mn = sb("mn", [P, NT * GROUPS, 1])
    m.ml = sb("ml", [P, NT * GROUPS, 1])
    m.t2 = sb("t2", [P, NT * GROUPS, 1])
    m.gs = sb("gs", [P, NT * GROUPS, 1])
    m.gt = sb("gt", [P, NT, GROUPS, GROUPS])
    m.eq = sb("eq", [P, NT, GROUPS, GROUPS])
    m.rk = sb("rk", [P, NT, GROUPS])
    m.cap = sb("cap", [P, NT * GROUPS])
    m.weight = sb("weight", [P, 2, NT])
    m.slot_f = sb("slot_f", [P, 2, NT])
    m.slots = sb("slots", [P, 2, 2, NT], U32)
    m.sel = sb("sel", [P, NT + 1, E], BF16)
    m.carry = sb("carry", [P, E])
    m.ci = sb("ci", [P, E], I32)
    m.cs = sb("cs", [P, E], I32)
    m.nt = sb("nt", [P, E])
    m.delta = sb("delta", [P, E])
    m.inc_a = sb("inc_a", [P, E])
    m.inc_b = sb("inc_b", [P, E])
    m.past = sb("past", [P, 2, E])
    m.past_d = sb("past_d", [P, 2, E])
    m.tabf = sb("tabf", [P, 4])
    m.tabr = sb("tabr", [P, 2])
    m.first = sb("first", [P, 2])
    m.pad_to = sb("pad_to", [P, E], I32)
    m.expert_of = sb("expert_of", [P, TILES])
    m.rf = sb("rf", [P, SLOTS, 2])
    m.rw0 = sb("rw0", [P, SLOTS])
    m.rw = sb("rw", [P, SLOTS])
    m.rdest = sb("rdest", [P, SLOTS], U32)
    m.xn = sb("xn", [P, NT, C])
    m.k_sb = sb("k_sb", [P, 2, C])
    m.v_sb = sb("v_sb", [P, 2, KC, P + 1])
    m.mix = sb("mix", [P, KC, P + CH])
    m.den = sb("den", [P, 2, KC, CH])
    m.z = sb("z", [P, 2, KC, CH])
    m.o_sb = sb("o_sb", [P, 2, C])
    m.oT = sb("oT", [P, 2, C])
    m.bank = [ctx.enter_context(nc.psum_tensor(f"bank{i}", [P, 512], FP32)) for i in range(8)]
    m.xs = [m.rows[:, h * NT * ROW:(h + 1) * NT * ROW].rearrange("p (i r) -> p i r", i=NT) for h in range(2)]
    m.yl = m.rows[:, 0:2 * NT * C].rearrange("p (k n) -> p k n", k=2)
    m.yl2 = m.w13[:, 0:2 * NT * C].rearrange("p (k n) -> p k n", k=2)

    def part(at, n, width):
        return m.rows[:, at:at + n * width].rearrange("p (n w) -> p n w", n=n)

    m.rin = part(0, SLOTS, ROW)
    m.rT = part(SLOTS * ROW, 2, C)
    m.rsilu = part(SLOTS * ROW + 2 * C, 2, INTER)
    m.rg = part(SLOTS * ROW + 2 * C + 2 * INTER, 2, INTER)
    m.rgT = part(SLOTS * ROW + 2 * C + 4 * INTER, 2, P)
    m.ry = m.xn
    m.table = m.xnT[0:1, 0, 0:2 * TQ].bitcast(I32)
    m.gT = m.work[:, 0:2 * HALF].rearrange("p (m n) -> p m n", m=2)
    m.silu = m.work[:, 2 * HALF:4 * HALF].rearrange("p (m n) -> p m n", m=2)
    m.qT = m.work[:, :].rearrange("p (m n) -> p m n", m=2)
    return m


def setup_stage(nc, m, d, sem):
    m.passed = sem("waits_passed")
    made, loaded, split, bounced, zeroed = (sem(n) for n in (
        "setup_pool_steps", "bias_loaded", "bias_split", "bias_bounced", "rows_zeroed"))
    placed, chain_s = sem("bias_placed"), sem("setup_dve_steps")
    nb = NBIAS // P
    bias_f = m.pos[:, :, :].rearrange("p i e -> p (i e)")[:, 0:nb]
    bias_r = m.ms[:, :, :].rearrange("p i e -> p (i e)")[:, 0:nb]
    parts = m.sel[:, :, :].rearrange("p i e -> p (i e)")
    parts2 = m.ones_b

    with nc.Block() as block:
        @block.sync
        def _(sp):
            sp.dma_start(bias_f, d.biases.rearrange("(p f) -> p f", p=P)).then_inc(loaded, 16)
            sp.wait_ge(split, 1)
            sp.dma_start(d.bias_parts[0].rearrange("(p f) -> p f", p=P), parts[:, 0:nb]).then_inc(bounced, 16)
            sp.wait_ge(split, 2)
            sp.dma_start(d.bias_parts[1].rearrange("(p f) -> p f", p=P), parts2[:, 0:nb]).then_inc(bounced, 16)
            sp.wait_ge(bounced, 32)
            sp.wait_ge(split, 3)
            sp.dma_start(d.bias_parts[2].rearrange("(p f) -> p f", p=P), parts[:, 0:nb]).then_inc(bounced, 16)
            sp.wait_ge(bounced, 48)
            sp.wait_ge(zeroed, 1)
            sp.dma_start(m.bias_rows[0:3, :], d.bias_parts).then_inc(placed, 16)
            sp.wait_ge(placed, 16)

        @block.vector
        def _(dve):
            ch = Chain(dve, chain_s)
            nc.vector.memset(m.bias_rows[:, :].bitcast(U32), 0).then_inc(zeroed, 1)
            dve.wait_ge(loaded, 16)
            nc.vector.tensor_copy(parts[:, 0:nb], bias_f).then_inc(split, 1)
            dve.wait_ge(split, 1)
            ch.then(nc.vector.tensor_tensor(bias_r, bias_f, parts[:, 0:nb], ALU.subtract))
            nc.vector.tensor_copy(parts2[:, 0:nb], bias_r).then_inc(split, 1)
            dve.wait_ge(split, 2)
            ch.then(nc.vector.tensor_tensor(bias_f, bias_r, parts2[:, 0:nb], ALU.subtract))
            dve.wait_ge(bounced, 32)
            nc.vector.tensor_copy(parts[:, 0:nb], bias_f).then_inc(split, 1)
            dve.wait_ge(bounced, 48)
            ch.then(nc.vector.memset(m.ones_b[:], 1.0))
            ch.then(nc.vector.memset(m.sel[:], 0.0))

        @block.gpsimd
        def _(pool):
            ch = Chain(pool, made)
            small = dict(allow_small_or_imprecise_dtypes=True)
            ch.did(nc.gpsimd.memset(m.ident[:], 0.0))
            ch.did(nc.gpsimd.memset(m.ones3[:], 0.0))
            ch.did(nc.gpsimd.memset(m.before[:], 0.0))
            ch.did(nc.gpsimd.memset(m.earlier[:], 0.0))
            ch.did(nc.gpsimd.memset(m.head_mask[:], 1.0))
            ch.did(nc.gpsimd.memset(m.minus_half[:], -0.5))
            ch.did(nc.gpsimd.memset(m.head_of[:], 1.0))
            ch.did(nc.gpsimd.memset(m.pad[:], 0.0))
            ch.did(nc.gpsimd.iota(m.rev[:], [[-1, E]], base=E, channel_multiplier=0, **small))
            ch.did(nc.gpsimd.iota(m.region0[:], [[REGION, E]], base=0, channel_multiplier=0, **small))
            ch.did(nc.gpsimd.iota(m.part[:], [[1, 1]], base=0, channel_multiplier=1, **small))
            ch.did(nc.gpsimd.iota(m.tile_no[:], [[P, 2]], base=0, channel_multiplier=1, **small))
            ch.settle()
            ch.did(nc.gpsimd.affine_select(out=m.ident[:], in_=m.ident[:], compare_op=ALU.not_equal, fill=1.0,
                                           base=0, pattern=[[-1, P]], channel_multiplier=1))
            ch.did(nc.gpsimd.affine_select(out=m.ones3[:], in_=m.ones3[:], compare_op=ALU.is_ge, fill=1.0,
                                           base=-3, pattern=[[0, P]], channel_multiplier=1))
            ch.did(nc.gpsimd.affine_select(out=m.before[:], in_=m.before[:], compare_op=ALU.is_ge, fill=1.0,
                                           base=0, pattern=[[-1, P]], channel_multiplier=1))
            ch.did(nc.gpsimd.affine_select(out=m.earlier[:], in_=m.earlier[:], compare_op=ALU.is_ge, fill=1.0,
                                           base=0, pattern=[[-1, GROUPS], [1, GROUPS]], channel_multiplier=0))
            hm = m.head_mask[:].rearrange("p (h d) -> p h d", d=HD)
            ch.did(nc.gpsimd.affine_select(out=hm, in_=hm, compare_op=ALU.is_ge, fill=0.0, base=0,
                                           pattern=[[-HD, CH], [0, HD]], channel_multiplier=1))
            ch.did(nc.gpsimd.affine_select(out=m.head_of[:], in_=m.head_of[:], compare_op=ALU.is_ge, fill=0.0,
                                           base=0, pattern=[[-HD, CH]], channel_multiplier=1))
            ch.did(nc.gpsimd.memset(m.pad[:, C:C + 1], float(2 * TOKENS)))
            ch.did(nc.gpsimd.memset(m.pad[:, C + 1:C + 3], -1.0))
            ch.settle()
            ch.did(nc.gpsimd.affine_select(out=hm, in_=hm, compare_op=ALU.is_ge, fill=0.0, base=HD - 1,
                                           pattern=[[HD, CH], [0, HD]], channel_multiplier=-1))
            ch.did(nc.gpsimd.affine_select(out=m.head_of[:], in_=m.head_of[:], compare_op=ALU.is_ge, fill=0.0,
                                           base=HD - 1, pattern=[[HD, CH]], channel_multiplier=-1))
            ch.settle()


ROUTE_STEPS = 35
META_STEPS = 6


def ffn_route_stage(nc, m, d, sem, layer):
    s = Names()
    s.stats_ready = sem(f"stats_ready{layer}")
    s.rstd_ready = sem(f"rstd_ready{layer}")
    s.xn_ready = sem(f"xn_ready{layer}")
    s.xT_ready = sem(f"xT_ready{layer}")
    s.xT_copied = sem(f"xT_copied{layer}")
    s.logits_ready = sem(f"logits_ready{layer}")
    s.shift_ready = sem(f"shift_ready{layer}")
    s.exp_ready = sem(f"exp_ready{layer}")
    s.sel_ready = sem(f"sel_ready{layer}")
    s.rank_ready = sem(f"rank_ready{layer}")
    s.rank_read = sem(f"rank_read{layer}")
    s.h1_ready = sem(f"h1_ready{layer}")
    s.h3_ready = sem(f"h3_ready{layer}")
    s.silu_ready = sem(f"silu_ready{layer}")
    s.gated_ready = sem(f"gated_ready{layer}")
    s.y_ready = sem(f"y_ready{layer}")
    s.y_added = sem(f"y_added{layer}")
    s.weights_ready = sem(f"weights_ready{layer}")
    s.slots_ready = sem(f"slots_ready{layer}")
    s.counts_ready = sem(f"counts_ready{layer}")
    s.pads_ready = sem(f"pads_ready{layer}")
    s.rows_ready = sem(f"rows_ready{layer}")
    s.table_ready = sem(f"table_ready{layer}")
    s.route_steps = sem(f"route_steps{layer}")
    s.meta_steps = sem(f"meta_steps{layer}")
    s.meta_written = sem(f"meta_written{layer}")
    scattered = [sem(f"scattered{layer}_{h}") for h in range(2)]
    padded = sem(f"padded{layer}")
    if layer == 0:
        x_in, weights_in = sem("x_in"), sem("ffn_weights_in")
        later_in, spare_out = sem("later_weights_in"), sem("spare_out")
        loads = [(m.gate_w[:], d.gate_w), (m.gate_b[:], d.gate_b), (m.ws1[:], d.ws1), (m.ws3[:], d.ws3),
                 (m.ws2[:], d.ws2), (m.bs1[:], d.bs1), (m.bs3[:], d.bs3)]
    xT_ps, logits_ps, rank_ps = m.bank[0:2], m.bank[2], m.bank[3]
    h1_ps, h3_ps = m.bank[4:6], m.bank[6:8]
    y_ps = [h1_ps[0], h3_ps[0]]
    logits = logits_ps[:, 0:NT * E].rearrange("p (i e) -> p i e", e=E)
    ranks = rank_ps[:, 0:(NT + 1) * E].rearrange("p (i e) -> p i e", e=E)

    def batches(eng, body):
        body(At(0, n=2))
        body(At(1, n=2))
        with eng.Fori(1, BATCHES // 2 - 1) as q:
            body(At(0, q, n=2))
            body(At(1, q, n=2))
        body(At(BATCHES - 2, n=2))
        body(At(BATCHES - 1, n=2))

    def is_last(b):
        return isinstance(b.q, int) and b.k == BATCHES - 1

    with nc.Block() as block:
        def load_all(sp):
            xv = d.x.rearrange("b (p j) c -> b p (j c)", p=P)
            sp.dma_start(m.xres[:, 0, :, :].rearrange("p j c -> p (j c)"), xv[0]).then_inc(x_in, 16)
            for dst, src in loads:
                sp.dma_start(dst, src).then_inc(weights_in, 16)
            sp.wait_ge(x_in, 16)
            with sp.Fori(1, BATCHES) as b:
                sp.dma_start(m.xres[:, bass.ds(b, 1), :, :].rearrange("p b j c -> p (b j c)"),
                             xv[bass.ds(b, 1)].rearrange("b p n -> (b p) n")).then_inc(x_in, 16)
                sp.wait_ge(x_in, b * 16 + 16)
                apart(sp, m.passed)
            for dst, src in ((m.w13[:], d.w13), (m.w2[:], d.w2), (m.w_qkv[:], d.w_qkv), (m.w_proj[:], d.w_proj)):
                sp.dma_start(dst, src).then_inc(later_in, 16)
            for i in range(SPARE_TILES):
                sp.dma_start(d.xg[SPARE + i * P:SPARE + (i + 1) * P, :], m.pad[:]).then_inc(spare_out, 16)
            sp.wait_ge(weights_in, 16 * len(loads))
            sp.wait_ge(later_in, 64)
            sp.wait_ge(spare_out, 16 * SPARE_TILES)

        @block.sync
        def _(sp):
            if layer == 0:
                load_all(sp)
            sp.wait_ge(s.pads_ready, 1)
            _, starts = nc.values_load_multi_w_load_instructions(
                m.pad_to[0:1, :], engines=(sp.engine,), min_val=0, max_val=SPARE - P,
                skip_runtime_bounds_check_because="a region holds a row for every token and a tile more")
            for start in starts:
                sp.dma_start(d.xg[bass.ds(start, P), :], m.pad[:]).then_inc(padded, 16)
            sp.wait_ge(padded, 16 * E)

        @block.tensor
        def _(pe):
            def transpose(b):
                wait(pe, s.xn_ready, b.times(1, 1))
                for n in range(4):
                    g, c = divmod(n, KC)
                    wait(pe, s.xT_copied, b.times(4, n - 1))
                    for j in range(4):
                        last = nc.tensor.transpose(xT_ps[n % 2][:, j * P:(j + 1) * P],
                                                   m.xs[b.slot(2)][:, 4 * g + j, c * P:(c + 1) * P], m.ident[:])
                    last.then_inc(s.xT_ready, 1)

            def gate(b):
                wait(pe, s.xT_copied, b.times(4, 4))
                for i in range(NT):
                    for c in range(KC):
                        last = nc.tensor.matmul(logits_ps[:, i * E:(i + 1) * E], m.xnT[:, c, i * P:(i + 1) * P],
                                                m.gate_w[:, c, :], start=c == 0, stop=c == KC - 1)
                last.then_inc(s.logits_ready, 1)

            def up(b, u):
                g, mi = divmod(u, 2)
                for ws, bank, ready, y in ((m.ws1, h1_ps[mi], s.h1_ready, 0), (m.ws3, h3_ps[mi], s.h3_ready, 1)):
                    if mi == 0:
                        wait(pe, s.y_added, b.times(4, 2 * g - 1 + y))
                    for c in range(KC):
                        last = nc.tensor.matmul(bank[:], ws[:, c, mi * P:(mi + 1) * P],
                                                m.xnT[:, c, g * HALF:(g + 1) * HALF],
                                                start=c == 0, stop=c == KC - 1)
                    last.then_inc(ready, 1)

            def down(b, g):
                wait(pe, s.gated_ready, b.times(4, 2 * g + 2))
                for q in range(2):
                    for t in range(2):
                        y = y_ps[q][:, t * C:(t + 1) * C]
                        for mi in range(KC):
                            nc.tensor.matmul(y, m.gT[:, mi, (2 * q + t) * P:(2 * q + t + 1) * P],
                                             m.ws2[:, mi, :], start=mi == 0, stop=False)
                        last = nc.tensor.matmul(y, m.ones3[:], m.bias_rows[:, BS2:BS2 + C], start=False, stop=True)
                    last.then_inc(s.y_ready, 1)

            def rank(b):
                wait(pe, s.sel_ready, b.times(1, 1))
                wait(pe, s.rank_read, b.times(1))
                nc.tensor.matmul(rank_ps[:, 0:(NT + 1) * E], m.before[:],
                                 m.sel[:].rearrange("p i e -> p (i e)"), start=True, stop=False)
                for i in range(NT):
                    last = nc.tensor.matmul(ranks[:, i + 1:, :], m.ones_b[:],
                                            m.sel[:, i:i + 1, :].to_broadcast([P, NT - i, E]),
                                            start=False, stop=i == NT - 1)
                last.then_inc(s.rank_ready, 1)

            if layer == 0:
                pe.wait_ge(weights_in, 16 * len(loads))
            transpose(At(0, n=2))

            def body(b):
                gate(b)
                up(b, 0)
                up(b, 1)
                down(b, 0)
                up(b, 2)
                rank(b)
                up(b, 3)
                if not is_last(b):
                    transpose(b + 1)
                down(b, 1)

            batches(pe, body)

            pe.wait_ge(s.table_ready, 1)
            for n in range(4):
                last = nc.tensor.matmul(xT_ps[0][:, n * P:(n + 1) * P], m.tabf[:, n:n + 1].to_broadcast([P, P]),
                                        m.ident[:], start=True, stop=True)
            last.then_inc(s.rows_ready, 1)

        @block.scalar
        def _(act):
            def normalise(b):
                wait(act, s.rstd_ready, b.times(1, 1))
                for i in range(NT):
                    last = nc.scalar.activation(
                        m.xs[b.slot(2)][:, i, 0:C], m.xres[:, bass.ds(b.times(1), 1), i, :].rearrange("p b c -> p (b c)"),
                        ACT.Identity, bias=m.nmr[:, i:i + 1], scale=m.rstd[:, i:i + 1])
                last.then_inc(s.xn_ready, 1)

            def copy_xT(b):
                for n in range(4):
                    g, c = divmod(n, KC)
                    wait(act, s.xT_ready, b.times(4, n + 1))
                    nc.scalar.copy(m.xnT[:, c, g * HALF:(g + 1) * HALF], xT_ps[n % 2][:]).then_inc(s.xT_copied, 1)

            def silu(b, u):
                mi = u % 2
                wait(act, s.h1_ready, b.times(4, u + 1))
                nc.scalar.activation(m.silu[:, mi, :], h1_ps[mi][:], ACT.Silu,
                                     bias=m.bs1[:, mi:mi + 1]).then_inc(s.silu_ready, 1)

            def body(b):
                wait(act, s.shift_ready, b.times(1, 1))
                nc.scalar.activation(m.ex[:], m.sh[:], ACT.Exp).then_inc(s.exp_ready, 1)
                silu(b, 0)
                silu(b, 1)
                silu(b, 2)
                if not is_last(b):
                    normalise(b + 1)
                silu(b, 3)
                if not is_last(b):
                    copy_xT(b + 1)

            if layer == 0:
                act.wait_ge(weights_in, 16 * len(loads))
            normalise(At(0, n=2))
            copy_xT(At(0, n=2))
            batches(act, body)

        @block.vector
        def _(dve):
            def stats(b):
                if layer == 0:
                    wait(dve, x_in, b.times(16, 16))
                apart(dve, m.passed)
                for i in range(NT):
                    last = nc.vector.bn_stats(
                        m.stat[:, i, :], m.xres[:, bass.ds(b.times(1), 1), i, :].rearrange("p b c -> p (b c)"))
                return last

            def aggregate():
                for i in range(NT):
                    last = nc.vector.bn_aggr(m.mv[:, i, :], m.stat[:, i, :])
                last.then_inc(s.stats_ready, 1)

            def gated(b, u):
                mi = u % 2
                wait(dve, s.h3_ready, b.times(4, u + 1))
                wait(dve, s.silu_ready, b.times(4, u + 1))
                nc.vector.scalar_tensor_tensor(m.gT[:, mi, :], h3_ps[mi][:], m.bs3[:, mi:mi + 1], m.silu[:, mi, :],
                                               ALU.add, ALU.mult).then_inc(s.gated_ready, 1)

            def add_shared(b, k):
                wait(dve, s.y_ready, b.times(4, k + 1))
                x = m.xres[:, bass.ds(b.times(1), 1), 2 * k:2 * k + 2, :].rearrange("p b t c -> p (b t c)")
                nc.vector.scalar_tensor_tensor(x, y_ps[k % 2][:], 0.5, x, ALU.mult, ALU.add).then_inc(s.y_added, 1)

            def per_tile(ap):
                return ap.rearrange("p (i o) -> p i o", o=1).to_broadcast([P, NT, E])

            def per_expert(ap):
                return ap[:].rearrange("p (o e) -> p o e", o=1).to_broadcast([P, NT, E])

            TT, TR = nc.vector.tensor_tensor, nc.vector.tensor_reduce

            def scores(b, ch):
                wait(dve, s.logits_ready, b.times(1, 1))
                ch.then(TR(m.mx[:], logits, AX.X, ALU.max))
                TT(m.sh[:], logits, per_tile(m.mx[:]), ALU.subtract).then_inc(s.shift_ready, 1)

            def groups(b, ch):
                wait(dve, s.exp_ready, b.times(1, 1))
                ch.then(TR(m.sm[:], m.ex[:], AX.X, ALU.add))
                ch.then(nc.vector.reciprocal(m.rs[:], m.sm[:]))
                ch.then(TT(m.pr[:], m.ex[:], per_tile(m.rs[:]), ALU.mult))
                ch.then(TT(m.sc[:], m.pr[:], per_expert(m.gate_b), ALU.add))
                pairs = m.sc[:].rearrange("p i (g u v) -> p (i g) u v", u=2, v=2)
                ch.did(TT(m.hi[:], pairs[:, :, :, 0], pairs[:, :, :, 1], ALU.max))
                ch.then(TT(m.lo[:], pairs[:, :, :, 0], pairs[:, :, :, 1], ALU.min))
                ch.did(TT(m.t1[:], m.hi[:, :, 0:1], m.hi[:, :, 1:2], ALU.max))
                ch.did(TT(m.mn[:], m.hi[:, :, 0:1], m.hi[:, :, 1:2], ALU.min))
                ch.then(TT(m.ml[:], m.lo[:, :, 0:1], m.lo[:, :, 1:2], ALU.max))
                ch.then(TT(m.t2[:], m.mn[:], m.ml[:], ALU.max))
                ch.then(TT(m.gs[:], m.t1[:], m.t2[:], ALU.add))

            def group_mask(b, ch):
                mine = m.gs[:].rearrange("p (i g) o -> p i g o", g=GROUPS).to_broadcast([P, NT, GROUPS, GROUPS])
                other = m.gs[:].rearrange("p (i g) o -> p i o g", g=GROUPS).to_broadcast([P, NT, GROUPS, GROUPS])
                earlier = m.earlier[:].rearrange("p (o g) h -> p o g h", o=1).to_broadcast([P, NT, GROUPS, GROUPS])
                ch.did(TT(m.gt[:], other, mine, ALU.is_gt))
                ch.then(TT(m.eq[:], other, mine, ALU.is_equal))
                ch.then(TT(m.eq[:], m.eq[:], earlier, ALU.mult))
                ch.then(TT(m.gt[:], m.gt[:], m.eq[:], ALU.add))
                ch.then(TR(m.rk[:], m.gt[:], AX.X, ALU.add))
                ch.then(nc.vector.tensor_scalar(m.cap[:], m.rk[:].rearrange("p i g -> p (i g)"), 1.5, -2e38,
                                                ALU.subtract, ALU.mult))
                ch.then(TT(m.ms[:].rearrange("p i (g u) -> p (i g) u", u=PER_GROUP),
                           m.sc[:].rearrange("p i (g u) -> p (i g) u", u=PER_GROUP),
                           m.cap[:].rearrange("p (n o) -> p n o", o=1).to_broadcast([P, NT * GROUPS, PER_GROUP]),
                           ALU.min))

            def choose(ch, scores_ap, best, k):
                ch.then(TR(best[:], scores_ap, AX.X, ALU.max))
                ch.then(TT(m.e1[:], scores_ap, per_tile(best[:]), ALU.is_equal))
                ch.then(TT(m.e1[:], m.e1[:], per_expert(m.rev), ALU.mult))
                ch.then(TR(m.rr[:, k], m.e1[:], AX.X, ALU.max))
                ch.then(TT(m.chosen[:, k], per_expert(m.rev), per_tile(m.rr[:, k]), ALU.is_equal))

            def second(b, ch):
                ch.then(nc.vector.scalar_tensor_tensor(
                    m.ms2[:].rearrange("p i e -> p (i e)"), m.chosen[:, 0].rearrange("p i e -> p (i e)"), -3e38,
                    m.ms[:].rearrange("p i e -> p (i e)"), ALU.mult, ALU.add))
                choose(ch, m.ms2[:], m.m2, 1)
                TT(m.sel[:, 0:NT, :], m.chosen[:, 0], m.chosen[:, 1], ALU.add).then_inc(s.sel_ready, 1)

            def weights(b, ch):
                flat = m.prod[:].rearrange("p k i e -> p (k i) e")
                for k in range(2):
                    last = TT(m.prod[:, k], m.chosen[:, k], m.pr[:], ALU.mult)
                ch.then(last)
                TR(m.weight[:].rearrange("p k i -> p (k i)"), flat, AX.X, ALU.add).then_inc(s.weights_ready, 1)

            def slots(b, ch):
                wait(dve, s.rank_ready, b.times(1, 1))
                wait(dve, s.weights_ready, b.times(1, 1))
                ch.then(TT(m.pos[:], ranks[:, 0:NT, :], per_expert(m.carry), ALU.add))
                TT(m.carry[:], m.carry[:], ranks[:, NT, :], ALU.add).then_inc(s.rank_read, 1)
                for k in range(2):
                    last = TT(m.prod[:, k], m.chosen[:, k], m.pos[:], ALU.mult)
                ch.then(last)
                ch.then(TR(m.slot_f[:].rearrange("p k i -> p (k i)"), m.prod[:].rearrange("p k i e -> p (k i) e"),
                           AX.X, ALU.add))
                nc.vector.tensor_copy(m.slots[:, b.slot(2)], m.slot_f[:]).then_inc(s.slots_ready, 1)
                wait(dve, s.rank_read, b.times(1, 1))

            def body(b):
                ch = Chain(dve, s.route_steps, b.times(ROUTE_STEPS, 1))
                scores(b, ch)
                groups(b, ch)
                gated(b, 0)
                if is_last(b):
                    ch.then(nc.vector.tensor_copy(m.first[:], m.tile_no[:]))
                else:
                    ch.then(stats(b + 1))
                    wait(dve, s.rstd_ready, b.times(1, 1))
                    apart(dve, m.passed)
                    aggregate()
                gated(b, 1)
                group_mask(b, ch)
                add_shared(b, 0)
                wait(dve, s.meta_written, b.times(1))
                choose(ch, m.ms[:], m.m1, 0)
                add_shared(b, 1)
                second(b, ch)
                weights(b, ch)
                gated(b, 2)
                slots(b, ch)
                gated(b, 3)
                add_shared(b, 2)
                add_shared(b, 3)
                assert ch.n == ROUTE_STEPS, ch.n

            ch = Chain(dve, s.route_steps)
            if layer == 0:
                dve.wait_ge(weights_in, 16 * len(loads))
            nc.vector.tensor_copy(m.carry[:], m.region0[:])
            ch.then(stats(At(0, n=2)))
            aggregate()
            batches(dve, body)

            ch = Chain(dve, s.route_steps, BATCHES * ROUTE_STEPS + 1)
            dve.wait_ge(s.rank_read, BATCHES)
            nc.vector.tensor_copy(m.pad_to[:], m.carry[:]).then_inc(s.pads_ready, 1)
            ch.then(TT(m.nt[:], m.carry[:], m.region0[:], ALU.subtract))
            ch.then(nc.vector.tensor_scalar(m.ci[:], m.nt[:], float(P - 1), None, ALU.add))
            ch.then(nc.vector.tensor_scalar(m.cs[:], m.ci[:], 7, None, ALU.arith_shift_right))
            ch.then(nc.vector.tensor_copy(m.nt[:], m.cs[:]))
            ch.did(nc.vector.tensor_scalar(m.delta[:], m.nt[:], float(-P), float(REGION), ALU.mult, ALU.add))
            a, b_, step = m.nt, m.inc_a, 1
            while step < E:
                ch.did(nc.vector.tensor_copy(b_[:, 0:step], a[:, 0:step]))
                ch.then(TT(b_[:, step:], a[:, step:], a[:, 0:E - step], ALU.add))
                a, b_, step = b_, (m.inc_b if b_ is m.inc_a else m.inc_a), 2 * step
            inc = a[:].rearrange("p (o e) -> p o e", o=1).to_broadcast([P, 2, E])
            no = m.tile_no[:].rearrange("p (j o) -> p j o", o=1).to_broadcast([P, 2, E])
            ch.then(TT(m.past[:], no, inc, ALU.is_ge))
            ch.did(TR(m.tabr[:], m.past[:], AX.X, ALU.add))
            ch.then(TT(m.past_d[:], m.past[:], m.delta[:].rearrange("p (o e) -> p o e", o=1).to_broadcast([P, 2, E]),
                       ALU.mult))
            ch.did(nc.vector.tensor_scalar(m.tabf[:, 0:2], m.tabr[:], float(E - 1), float(C), ALU.min, ALU.mult))
            ch.then(TR(m.first[:], m.past_d[:], AX.X, ALU.add))
            nc.vector.scalar_tensor_tensor(m.tabf[:, 2:4], m.tile_no[:], float(P), m.first[:], ALU.mult,
                                           ALU.add).then_inc(s.table_ready, 1)
            dve.wait_ge(s.rows_ready, 1)
            nc.vector.tensor_copy(m.table, xT_ps[0][0:1, :])
            nc.vector.tensor_scalar(m.expert_of[:], xT_ps[0][:, 0:TILES], 1.0 / C, None, ALU.mult)

        @block.gpsimd
        def _(pool):
            def rstd(b, ch):
                wait(pool, s.stats_ready, b.times(1, 1))
                wait(pool, scattered[b.slot(2)], b.turn(2, 16 * 2 * NT))
                apart(pool, m.passed)
                ch.then(nc.gpsimd.tensor_scalar(m.ve[:], m.mv[:, :, 1], LN_EPS, None, ALU.add))
                ch.then(nc.gpsimd.tensor_tensor(m.rstd[:], m.ve[:], m.minus_half[:], ALU.pow))
                ch.then(nc.gpsimd.tensor_tensor(m.mr[:], m.mv[:, :, 0], m.rstd[:], ALU.mult))
                nc.gpsimd.tensor_scalar(m.nmr[:], m.mr[:], -1.0, None, ALU.mult).then_inc(s.rstd_ready, 1)

            def body(b):
                ch = Chain(pool, s.meta_steps, b.times(META_STEPS, 3), m.passed)
                if not is_last(b):
                    rstd(b + 1, ch)
                xs = m.xs[b.slot(2)]
                wait(pool, s.xn_ready, b.times(1, 1))
                wait(pool, s.weights_ready, b.times(1, 1))
                apart(pool, m.passed)
                ch.did(nc.gpsimd.tensor_copy(xs[:, :, C:C + 1], m.tok[:].rearrange("p (i o) -> p i o", o=1)))
                ch.did(nc.gpsimd.tensor_scalar(xs[:, :, C + 1:C + 3], m.rr[:].rearrange("p k i -> p i k"),
                                               -1.0, float(E), ALU.mult, ALU.add))
                ch.then(nc.gpsimd.tensor_scalar(xs[:, :, C + 3:C + 5], m.weight[:].rearrange("p k i -> p i k"),
                                                0.5, None, ALU.mult))
                nc.gpsimd.tensor_scalar(m.tok[:], m.tok[:], float(SEQ), None, ALU.add).then_inc(s.meta_written, 1)
                wait(pool, s.slots_ready, b.times(1, 1))
                apart(pool, m.passed)
                for k in range(2):
                    for i in range(NT):
                        nc.gpsimd.indirect_dma_start(
                            out=d.xg, out_offset=bass.IndirectOffsetOnAxis(ap=m.slots[:, b.slot(2), k, i:i + 1], axis=0),
                            in_=xs[:, i, :], in_offset=None).then_inc(scattered[b.slot(2)], 16)

            small = dict(allow_small_or_imprecise_dtypes=True)
            nc.gpsimd.iota(m.tok[:], [[1, NT]], base=0, channel_multiplier=NT, **small)
            rstd(At(0, n=2), Chain(pool, s.meta_steps, 0, m.passed))
            batches(pool, body)
            for h in range(2):
                pool.wait_ge(scattered[h], 16 * NT * BATCHES)


def routed_stage(nc, m, d, sem, layer):
    s = Names()
    s.rT_ready = sem(f"rT_ready{layer}")
    s.rT_copied = sem(f"rT_copied{layer}")
    s.rh_ready = sem(f"rh_ready{layer}")
    s.rsilu_ready = sem(f"rsilu_ready{layer}")
    s.rgated_ready = sem(f"rgated_ready{layer}")
    s.rgT_ready = sem(f"rgT_ready{layer}")
    s.rgT_copied = sem(f"rgT_copied{layer}")
    s.ry_ready = sem(f"ry_ready{layer}")
    s.ry_scaled = sem(f"ry_scaled{layer}")
    s.rmeta_ready = sem(f"rmeta_ready{layer}")
    s.rmeta_steps = sem(f"rmeta_steps{layer}")
    rows_in = [sem(f"rows_in{layer}_{n}") for n in range(SLOTS)]
    rows_out = [sem(f"rows_out{layer}_{n}") for n in range(SLOTS)]
    rT_ps, h_ps, gT_ps, y_ps = (m.bank[2 * n:2 * n + 2] for n in range(4))

    def steps(eng, step, begin=None):
        lo, hi = LOOPED
        for t in range(-1, lo):
            step(At(t))
        with eng.Fori(0, (hi - lo) // SLOTS) as q:
            if begin:
                begin(q)
            for r in range(SLOTS):
                step(At(lo + r, q, SLOTS))
        for t in range(hi, TILES + 2):
            step(At(t))

    def real(t):
        return not isinstance(t.q, int) or 0 <= t.k < TILES

    with nc.Block() as block:
        @block.sync
        def _(sp):
            def load(t):
                wait(sp, s.rT_ready, t.times(1, 1 - SLOTS))
                wait(sp, s.rmeta_ready, t.times(1, 1 - SLOTS))
                apart(sp, m.passed)
                row = sp.value_load(m.table[0:1, bass.ds(t.times(1, TQ), 1)], min_val=0, max_val=XG_ROWS - P)
                sp.dma_start(m.rin[:, t.slot(SLOTS), :], d.xg[bass.ds(row, P), :]).then_inc(rows_in[t.slot(SLOTS)], 16)

            steps(sp, lambda t: load(t) if real(t) else None)

        @block.tensor
        def _(pe):
            values = []

            def begin(q):
                _, loaded = nc.values_load_multi_w_load_instructions(
                    m.table[0:1, bass.ds(q * SLOTS + (LOOPED[0] - 2), SLOTS + 2)], engines=(pe.engine,),
                    min_val=0, max_val=(E - 1) * C, skip_runtime_bounds_check_because="the table's making bounds them")
                values[:] = loaded

            def weights_at(t):
                if not isinstance(t.q, int):
                    return values[t.k - (LOOPED[0] - 2)]
                return pe.value_load(m.table[0:1, t.k:t.k + 1], min_val=0, max_val=(E - 1) * C)

            def step(t):
                a = t + 1
                if real(a):
                    wait(pe, rows_in[a.slot(SLOTS)], a.turn(SLOTS, 16, 16))
                    wait(pe, s.rT_copied, a.times(1, -1))
                    for c in range(KC):
                        last = nc.tensor.transpose(rT_ps[a.slot(2)][:, c * P:(c + 1) * P],
                                                   m.rin[:, a.slot(SLOTS), c * P:(c + 1) * P], m.ident[:])
                    last.then_inc(s.rT_ready, 1)
                if real(t):
                    e = weights_at(t)
                    wait(pe, s.rT_copied, t.times(1, 1))
                    wait(pe, s.rgated_ready, t.times(1, -1))
                    h = h_ps[t.slot(2)][:, 0:2 * INTER]
                    for c in range(KC):
                        nc.tensor.matmul(h, m.rT[:, t.slot(2), c * P:(c + 1) * P],
                                         m.w13[:, c * E * C:(c + 1) * E * C][:, bass.ds(e, C)],
                                         start=c == 0, stop=False)
                    nc.tensor.matmul(h, m.ones3[:], m.bias_rows[:, BE13:BE13 + E * C][:, bass.ds(e, C)],
                                     start=False, stop=True).then_inc(s.rh_ready, 1)
                g = t + -1
                if real(g):
                    wait(pe, s.rgated_ready, g.times(1, 1))
                    wait(pe, s.rgT_copied, g.times(1, -1))
                    nc.tensor.transpose(gT_ps[g.slot(2)][:, 0:P], m.rg[:, g.slot(2), :],
                                        m.ident[:]).then_inc(s.rgT_ready, 1)
                y = t + -2
                if real(y):
                    e = weights_at(y)
                    wait(pe, s.rgT_copied, y.times(1, 1))
                    wait(pe, s.ry_scaled, y.times(1, -1))
                    nc.tensor.matmul(y_ps[y.slot(2)][:, 0:C], m.rgT[:, y.slot(2), :],
                                     m.w2[:, bass.ds(e, C)], start=True, stop=False)
                    nc.tensor.matmul(y_ps[y.slot(2)][:, 0:C], m.ones3[:],
                                     m.bias_rows[:, BE2:BE2 + E * C][:, bass.ds(e, C)],
                                     start=False, stop=True).then_inc(s.ry_ready, 1)

            steps(pe, step, begin)

        @block.scalar
        def _(act):
            def step(t):
                a = t + 1
                if real(a):
                    wait(act, s.rT_ready, a.times(1, 1))
                    wait(act, s.rh_ready, a.times(1, -1))
                    nc.scalar.copy(m.rT[:, a.slot(2), :], rT_ps[a.slot(2)][:, 0:C]).then_inc(s.rT_copied, 1)
                g = t + -1
                if real(t):
                    wait(act, s.rh_ready, t.times(1, 1))
                    wait(act, s.rgated_ready, t.times(1, -1))
                    nc.scalar.activation(m.rsilu[:, t.slot(2), :], h_ps[t.slot(2)][:, 0:INTER],
                                         ACT.Silu).then_inc(s.rsilu_ready, 1)
                if real(g):
                    wait(act, s.rgT_ready, g.times(1, 1))
                    wait(act, s.ry_ready, g.times(1, -1))
                    nc.scalar.copy(m.rgT[:, g.slot(2), :], gT_ps[g.slot(2)][:, 0:P]).then_inc(s.rgT_copied, 1)

            steps(act, step)

        @block.vector
        def _(dve):
            def step(t):
                a, y = t + 1, t + -2
                n = a.slot(SLOTS)
                r, flag = m.rin[:, n, :], m.rf[:, n, :]
                ch = Chain(dve, s.rmeta_steps, a.times(2))
                if real(a):
                    wait(dve, rows_in[n], a.turn(SLOTS, 16, 16))
                    wait(dve, rows_out[n], a.turn(SLOTS, 16))
                    ch.did(nc.vector.tensor_tensor(flag, r[:, C + 1:C + 3],
                                                   m.expert_of[:, bass.ds(a.times(1), 1)].to_broadcast([P, 2]),
                                                   ALU.is_equal))
                if real(t):
                    wait(dve, s.rsilu_ready, t.times(1, 1))
                    wait(dve, s.rgT_ready, t.times(1, -1))
                    nc.vector.tensor_tensor(m.rg[:, t.slot(2), :], h_ps[t.slot(2)][:, INTER:2 * INTER],
                                            m.rsilu[:, t.slot(2), :], ALU.mult).then_inc(s.rgated_ready, 1)
                if real(a):
                    ch.settle()
                    nc.vector.tensor_scalar(m.rdest[:, n:n + 1], flag[:, 1:2], float(TOKENS), r[:, C:C + 1],
                                            ALU.mult, ALU.add)
                    ch.did(nc.vector.tensor_scalar(m.rw0[:, n:n + 1], flag[:, 0:1], r[:, C + 3:C + 4], None, ALU.mult))
                if real(y):
                    wait(dve, s.ry_ready, y.times(1, 1))
                    wait(dve, s.rmeta_ready, y.times(1, 1))
                    wait(dve, rows_out[y.slot(SLOTS)], y.turn(SLOTS, 16))
                    nc.vector.tensor_scalar(m.ry[:, y.slot(SLOTS), :], y_ps[y.slot(2)][:, 0:C],
                                            m.rw[:, y.slot(SLOTS):y.slot(SLOTS) + 1], None,
                                            ALU.mult).then_inc(s.ry_scaled, 1)
                if real(a):
                    ch.settle()
                    nc.vector.scalar_tensor_tensor(m.rw[:, n:n + 1], flag[:, 1:2], r[:, C + 4:C + 5],
                                                   m.rw0[:, n:n + 1], ALU.mult, ALU.add).then_inc(s.rmeta_ready, 1)

            steps(dve, step)

        @block.gpsimd
        def _(pool):
            def scatter(y):
                wait(pool, s.ry_scaled, y.times(1, 1))
                wait(pool, s.rmeta_ready, y.times(1, 1))
                apart(pool, m.passed)
                nc.gpsimd.indirect_dma_start(
                    out=d.yt, out_offset=bass.IndirectOffsetOnAxis(ap=m.rdest[:, y.slot(SLOTS):y.slot(SLOTS) + 1], axis=0),
                    in_=m.ry[:, y.slot(SLOTS), :], in_offset=None,
                    bounds_check=2 * TOKENS - 1, oob_is_err=False).then_inc(rows_out[y.slot(SLOTS)], 16)

            steps(pool, lambda t: scatter(t + -2) if real(t + -2) else None)
            for n in range(SLOTS):
                pool.wait_ge(rows_out[n], 16 * (TILES // SLOTS))


def attention_stage(nc, m, d, sem):
    s = Names()
    s.routed_in = sem("routed_in")
    s.combined = sem("combined")
    s.a_stats_ready = sem("a_stats_ready")
    s.a_rstd_ready = sem("a_rstd_ready")
    s.a_xn_ready = sem("a_xn_ready")
    s.a_xT_ready = sem("a_xT_ready")
    s.a_xT_copied = sem("a_xT_copied")
    s.kv_ready = sem("kv_ready")
    s.kv_copied = sem("kv_copied")
    s.ctx_ready = sem("ctx_ready")
    s.mixer_ready = sem("mixer_ready")
    s.q_ready = sem("q_ready")
    s.q_copied = sem("q_copied")
    s.out_ready = sem("out_ready")
    s.out_scaled = sem("out_scaled")
    s.oT_ready = sem("oT_ready")
    s.oT_copied = sem("oT_copied")
    s.proj_ready = sem("proj_ready")
    s.proj_added = sem("proj_added")
    s.a_steps = sem("a_steps")
    s.a_rstd_steps = sem("a_rstd_steps")
    s.v_ones = sem("v_ones")
    xT_ps, kv_ps, ctx_ps, q_ps = (m.bank[2 * n:2 * n + 2] for n in range(4))
    out_ps, oT_ps, proj_ps = kv_ps, ctx_ps, q_ps
    xn = m.xn
    W = P + CH

    def batches(eng, body):
        body(At(0, n=1))
        with eng.Fori(1, BATCHES - 1) as q:
            body(At(0, q, n=1))
        body(At(BATCHES - 1, n=1))

    def is_last(b):
        return isinstance(b.q, int) and b.k == BATCHES - 1

    with nc.Block() as block:
        @block.sync
        def _(sp):
            yv = d.yt.rearrange("(k b p j) c -> b p k (j c)", k=2, b=BATCHES, p=P)

            def load(b):
                wait(sp, s.combined, b.times(1))
                sp.dma_start(m.yl, yv[bass.ds(b.times(1), 1)].rearrange("b p k n -> (b p) k n")
                             ).then_inc(s.routed_in, 16)

            batches(sp, load)

        @block.tensor
        def _(pe):
            def transpose(b):
                wait(pe, s.a_xn_ready, b.times(1, 1))
                for n in range(4):
                    g, c = divmod(n, KC)
                    wait(pe, s.a_xT_copied, b.times(4, n - 1))
                    for j in range(4):
                        last = nc.tensor.transpose(xT_ps[n % 2][:, j * P:(j + 1) * P],
                                                   xn[:, 4 * g + j, c * P:(c + 1) * P], m.ident[:])
                    last.then_inc(s.a_xT_ready, 1)

            def keys_values(b, i):
                wait(pe, s.kv_copied, b.times(NT, i - 1))
                wait(pe, s.out_scaled, b.times(NT))
                for c in range(KC):
                    last = nc.tensor.matmul(kv_ps[i % 2][:], m.xnT[:, c, i * P:(i + 1) * P],
                                            m.w_qkv[:, c, C:3 * C], start=c == 0, stop=c == KC - 1)
                last.then_inc(s.kv_ready, 1)

            def context(b, i):
                wait(pe, s.kv_copied, b.times(NT, i + 1))
                wait(pe, s.oT_copied, b.times(NT))
                for c in range(KC):
                    last = nc.tensor.matmul(ctx_ps[c][:, 0:P + 1], m.k_sb[:, i % 2, c * P:(c + 1) * P],
                                            m.v_sb[:, i % 2, c, :], start=i == 0, stop=i == NT - 1)
                last.then_inc(s.ctx_ready, 1)

            def queries(b):
                for n in range(4):
                    g, mi = divmod(n, 2)
                    wait(pe, s.q_copied, b.times(4, n - 1))
                    wait(pe, s.proj_added, b.times(NT))
                    for c in range(KC):
                        last = nc.tensor.matmul(q_ps[n % 2][:], m.w_qkv[:, c, mi * P:(mi + 1) * P],
                                                m.xnT[:, c, g * HALF:(g + 1) * HALF],
                                                start=c == 0, stop=c == KC - 1)
                    last.then_inc(s.q_ready, 1)

            def outputs(b, i):
                wait(pe, s.out_scaled, b.times(NT, i - 1))
                for c in range(KC):
                    last = nc.tensor.matmul(out_ps[i % 2][:, c * W:(c + 1) * W], m.qT[:, c, i * P:(i + 1) * P],
                                            m.mix[:, c, :], start=True, stop=True)
                last.then_inc(s.out_ready, 1)

            def transpose_out(b, i):
                wait(pe, s.out_scaled, b.times(NT, i + 1))
                wait(pe, s.oT_copied, b.times(NT, i - 1))
                for c in range(KC):
                    last = nc.tensor.transpose(oT_ps[i % 2][:, c * P:(c + 1) * P],
                                               m.o_sb[:, i % 2, c * P:(c + 1) * P], m.ident[:])
                last.then_inc(s.oT_ready, 1)

            def project(b, i):
                wait(pe, s.oT_copied, b.times(NT, i + 1))
                wait(pe, s.proj_added, b.times(NT, i - 1))
                for c in range(KC):
                    nc.tensor.matmul(proj_ps[i % 2][:, 0:C], m.oT[:, i % 2, c * P:(c + 1) * P], m.w_proj[:, c, :],
                                     start=c == 0, stop=False)
                nc.tensor.matmul(proj_ps[i % 2][:, 0:C], m.ones3[:], m.bias_rows[:, BPROJ:BPROJ + C],
                                 start=False, stop=True).then_inc(s.proj_ready, 1)

            def body(b):
                wait(pe, s.a_xT_copied, b.times(4, 4))
                for i in range(NT + 1):
                    if i < NT:
                        keys_values(b, i)
                    if i:
                        context(b, i - 1)
                queries(b)
                if not is_last(b):
                    transpose(b + 1)
                wait(pe, s.mixer_ready, b.times(1, 1))
                wait(pe, s.q_copied, b.times(4, 4))
                for i in range(NT + 2):
                    if i < NT:
                        outputs(b, i)
                    if 1 <= i <= NT:
                        transpose_out(b, i - 1)
                    if i >= 2:
                        project(b, i - 2)

            transpose(At(0, n=1))
            batches(pe, body)

        @block.scalar
        def _(act):
            def normalise(b, tiles):
                wait(act, s.a_rstd_ready, b.times(1, 1))
                for i in tiles:
                    last = nc.scalar.activation(
                        xn[:, i, :], m.xres[:, bass.ds(b.times(1), 1), i, :].rearrange("p b c -> p (b c)"),
                        ACT.Identity, bias=m.nmr[:, i:i + 1], scale=m.rstd[:, i:i + 1])
                if i == NT - 1:
                    last.then_inc(s.a_xn_ready, 1)

            def copy_xT(b):
                for n in range(4):
                    g, c = divmod(n, KC)
                    wait(act, s.a_xT_ready, b.times(4, n + 1))
                    nc.scalar.copy(m.xnT[:, c, g * HALF:(g + 1) * HALF], xT_ps[n % 2][:]).then_inc(s.a_xT_copied, 1)

            def body(b):
                if not is_last(b):
                    at = dict(zip(range(NT // 2 + 1, NT), (range(0, 3), range(3, 6), range(6, NT))))
                for i in range(NT):
                    wait(act, s.kv_ready, b.times(NT, i + 1))
                    wait(act, s.ctx_ready, b.times(NT, i - 1))
                    nc.scalar.activation(m.k_sb[:, i % 2, :], kv_ps[i % 2][:, 0:C], ACT.Relu)
                    nc.scalar.copy(m.v_sb[:, i % 2, :, 0:P],
                                   kv_ps[i % 2][:, C:2 * C].rearrange("p (c n) -> p c n", c=KC)
                                   ).then_inc(s.kv_copied, 1)
                    if not is_last(b) and i in at:
                        normalise(b + 1, at[i])
                for n in range(4):
                    g, mi = divmod(n, 2)
                    wait(act, s.q_ready, b.times(4, n + 1))
                    nc.scalar.activation(m.qT[:, mi, g * HALF:(g + 1) * HALF], q_ps[n % 2][:],
                                         ACT.Relu).then_inc(s.q_copied, 1)
                if not is_last(b):
                    copy_xT(b + 1)
                for i in range(NT):
                    wait(act, s.oT_ready, b.times(NT, i + 1))
                    wait(act, s.proj_ready, b.times(NT, i - 1))
                    nc.scalar.copy(m.oT[:, i % 2, :], oT_ps[i % 2][:, 0:C]).then_inc(s.oT_copied, 1)

            act.wait_ge(s.v_ones, 1)
            normalise(At(0, n=1), range(NT))
            copy_xT(At(0, n=1))
            batches(act, body)

        @block.vector
        def _(dve):
            STEPS = 2 + 2 * NT
            TT = nc.vector.tensor_tensor

            def combine(b, ch):
                x = m.xres[:, bass.ds(b.times(1), 1), :, :].rearrange("p b i c -> p (b i c)")
                wait(dve, s.routed_in, b.times(16, 16))
                ch.then(TT(x, x, m.yl[:, 0, :], ALU.add))
                TT(x, x, m.yl[:, 1, :], ALU.add).then_inc(s.combined, 1)
                wait(dve, s.combined, b.times(1, 1))
                apart(dve, m.passed)
                for i in range(NT):
                    last = nc.vector.bn_stats(
                        m.stat[:, i, :], m.xres[:, bass.ds(b.times(1), 1), i, :].rearrange("p b c -> p (b c)"))
                ch.did(last)
                ch.settle()
                wait(dve, s.a_rstd_ready, b.times(1))
                apart(dve, m.passed)
                for i in range(NT):
                    last = nc.vector.bn_aggr(m.mv[:, i, :], m.stat[:, i, :])
                last.then_inc(s.a_stats_ready, 1)

            def mixer(b):
                wait(dve, s.ctx_ready, b.times(NT, NT))
                for c in range(KC):
                    TT(m.mix[:, c, 0:P], ctx_ps[c][:, 0:P], m.head_mask[:], ALU.mult)
                    last = nc.vector.tensor_scalar(m.mix[:, c, P:W], m.head_of[:], ctx_ps[c][:, P:P + 1], None,
                                                   ALU.mult)
                last.then_inc(s.mixer_ready, 1)

            def scale(b, i, ch):
                wait(dve, s.out_ready, b.times(NT, i + 1))
                wait(dve, s.oT_ready, b.times(NT, i - 1))
                o = out_ps[i % 2][:, 0:KC * W].rearrange("p (c w) -> p c w", c=KC)
                ch.then(nc.vector.tensor_scalar(m.den[:, i % 2], o[:, :, P:W], EPS, None, ALU.add))
                ch.then(nc.vector.reciprocal(m.z[:, i % 2], m.den[:, i % 2]))
                TT(m.o_sb[:, i % 2, :].rearrange("p (c h d) -> p c h d", c=KC, h=CH),
                   o[:, :, 0:P].rearrange("p c (h d) -> p c h d", h=CH),
                   m.z[:, i % 2].rearrange("p c (h o) -> p c h o", o=1).to_broadcast([P, KC, CH, HD]),
                   ALU.mult).then_inc(s.out_scaled, 1)

            def add(b, i):
                wait(dve, s.proj_ready, b.times(NT, i + 1))
                x = m.xres[:, bass.ds(b.times(1), 1), i, :].rearrange("p b c -> p (b c)")
                TT(x, x, proj_ps[i % 2][:, 0:C], ALU.add).then_inc(s.proj_added, 1)

            nc.vector.memset(m.v_sb[:], 1.0).then_inc(s.v_ones, 1)
            combine(At(0, n=1), Chain(dve, s.a_steps))

            def body(b):
                ch = Chain(dve, s.a_steps, b.times(STEPS, 2))
                if not is_last(b):
                    combine(b + 1, ch)
                mixer(b)
                for i in range(NT + 2):
                    if i < NT:
                        scale(b, i, ch)
                    if i >= 2:
                        add(b, i - 2)

            batches(dve, body)

        @block.gpsimd
        def _(pool):
            def rstd(b):
                ch = Chain(pool, s.a_rstd_steps, b.times(3), m.passed)
                wait(pool, s.a_stats_ready, b.times(1, 1))
                wait(pool, s.a_xn_ready, b.times(1))
                apart(pool, m.passed)
                ch.then(nc.gpsimd.tensor_scalar(m.ve[:], m.mv[:, :, 1], LN_EPS, None, ALU.add))
                ch.then(nc.gpsimd.tensor_tensor(m.rstd[:], m.ve[:], m.minus_half[:], ALU.pow))
                ch.then(nc.gpsimd.tensor_tensor(m.mr[:], m.mv[:, :, 0], m.rstd[:], ALU.mult))
                nc.gpsimd.tensor_scalar(m.nmr[:], m.mr[:], -1.0, None, ALU.mult).then_inc(s.a_rstd_ready, 1)

            batches(pool, rstd)


def final_stage(nc, m, d, sem):
    routed_in = [sem(f"f_routed_in{h}") for h in range(2)]
    added, stored, steps_s = sem("f_added"), sem("f_stored"), sem("f_steps")
    buf = [m.yl, m.yl2]

    def batches(eng, body):
        body(At(0, n=2))
        body(At(1, n=2))
        with eng.Fori(1, BATCHES // 2) as q:
            body(At(0, q, n=2))
            body(At(1, q, n=2))

    with nc.Block() as block:
        @block.sync
        def _(sp):
            yv = d.yt.rearrange("(k b p j) c -> b p k (j c)", k=2, b=BATCHES, p=P)

            def load(b):
                wait(sp, added, b.times(1, -1))
                sp.dma_start(buf[b.slot(2)], yv[bass.ds(b.times(1), 1)].rearrange("b p k n -> (b p) k n")
                             ).then_inc(routed_in[b.slot(2)], 16)

            batches(sp, load)

        @block.vector
        def _(dve):
            def body(b):
                x = m.xres[:, bass.ds(b.times(1), 1), :, :].rearrange("p b i c -> p (b i c)")
                y = buf[b.slot(2)]
                wait(dve, routed_in[b.slot(2)], b.turn(2, 16, 16))
                Chain(dve, steps_s, b.times(1)).then(nc.vector.tensor_tensor(x, x, y[:, 0, :], ALU.add))
                nc.vector.tensor_tensor(x, x, y[:, 1, :], ALU.add).then_inc(added, 1)

            batches(dve, body)

        @block.scalar
        def _(act):
            ov = d.out.rearrange("b (p j) c -> b p (j c)", p=P)

            def store(b):
                wait(act, added, b.times(1, 1))
                act.dma_start(ov[bass.ds(b.times(1), 1)].rearrange("b p n -> (b p) n"),
                              m.xres[:, bass.ds(b.times(1), 1), :, :].rearrange("p b i c -> p (b i c)")
                              ).then_inc(stored, 16)

            batches(act, store)
            act.wait_ge(stored, 16 * BATCHES)


def build(nc, drams):
    d = Names()
    d.x = drams["x"]
    d.gate_w = drams["gate_w"]
    d.gate_b = drams["gate_b"]
    d.w13 = drams["w13"]
    d.w2 = drams["w2"]
    d.ws1 = drams["ws1"]
    d.ws3 = drams["ws3"]
    d.ws2 = drams["ws2"]
    d.bs1 = drams["bs1"]
    d.bs3 = drams["bs3"]
    d.w_qkv = drams["w_qkv"]
    d.w_proj = drams["w_proj"]
    d.biases = drams["biases"]
    d.out = drams["out"]
    d.xg = nc.dram_tensor("expert_rows", (XG_ROWS, ROW), FP32, kind="Internal").ap()
    d.yt = nc.dram_tensor("routed_rows", (2 * TOKENS, C), FP32, kind="Internal").ap()
    d.bias_parts = nc.dram_tensor("bias_parts", (3, NBIAS), BF16, kind="Internal").ap()
    with ExitStack() as ctx:
        m = allocate(nc, ctx)

        def sem(name):
            return ctx.enter_context(nc.semaphore(name))

        setup_stage(nc, m, d, sem)
        ffn_route_stage(nc, m, d, sem, 0)
        routed_stage(nc, m, d, sem, 0)
        attention_stage(nc, m, d, sem)
        ffn_route_stage(nc, m, d, sem, 1)
        routed_stage(nc, m, d, sem, 1)
        final_stage(nc, m, d, sem)


def kernel(**inputs):
    import concourse.bacc as _bacc
    from concourse.bass_utils import run_bass_kernel_spmd as _run

    a = {n: np.ascontiguousarray(v) for n, v in inputs.items()}
    f = "L0_ffn_"

    def chunks(w):
        return w.reshape(-1, P, w.shape[1]).transpose(1, 0, 2)

    w13 = np.concatenate([a[f + "We1"], a[f + "We3"]], axis=2)
    be13 = np.concatenate([a[f + "be1"], a[f + "be3"]], axis=1)
    laid = {
        "x": a["L0_attn_x"],
        "gate_w": chunks(a[f + "gate_w"].T),
        "gate_b": np.broadcast_to(a[f + "gate_b"], (P, E)),
        "w13": w13.reshape(E, KC, P, 2 * INTER).transpose(2, 1, 0, 3).reshape(P, -1),
        "w2": a[f + "We2"].transpose(1, 0, 2).reshape(P, -1),
        "ws1": chunks(a[f + "ws1"]),
        "ws3": chunks(a[f + "ws3"]),
        "ws2": chunks(a[f + "ws2"]),
        "bs1": a[f + "bs1"].reshape(KC, P).T,
        "bs3": a[f + "bs3"].reshape(KC, P).T,
        "w_qkv": chunks(a["L0_attn_w_qkv"].T),
        "w_proj": chunks(a["L0_attn_w_proj"].T),
        "biases": np.concatenate([be13.reshape(-1), a[f + "be2"].reshape(-1), a[f + "bs2"], a["L0_attn_b_proj"]]),
    }
    nc = _bacc.Bacc("TRN2", target_bir_lowering=False, num_devices=1)
    arrays = {}
    drams = {}
    for name, v in laid.items():
        v = np.ascontiguousarray(v)
        arrays[f"in_{name}"] = v
        drams[name] = nc.dram_tensor(f"in_{name}", v.shape, mybir.dt.from_np(v.dtype), kind="ExternalInput").ap()
    drams["out"] = nc.dram_tensor("out_0", (BATCHES, SEQ, C), FP32, kind="ExternalOutput").ap()
    build(nc, drams)
    r = _run(nc, [arrays], core_ids=[0])
    return r.results[0]["out_0"]
```

```python
from contextlib import ExitStack

import numpy as np

import concourse.bass as bass
from concourse import mybir

FP32, BF16 = mybir.dt.float32, mybir.dt.bfloat16
I32, U32 = mybir.dt.int32, mybir.dt.uint32
ALU, ACT, AX = mybir.AluOpType, mybir.ActivationFunctionType, mybir.AxisListType

P = 128
BATCHES, SEQ, C = 8, 1024, 256
TOKENS = BATCHES * SEQ
NT = SEQ // P
KC = C // P
E, GROUPS, INTER = 16, 4, 128
PER_GROUP = E // GROUPS
SHARED = 2 * INTER
HALF = SEQ // 2
HEADS, HD = 16, 16
CH = P // HD
LN_EPS = 1e-5
EPS = float(np.finfo(np.float32).eps)

ROW = C + 5
REGION = TOKENS + P
TILES = 2 * TOKENS // P + E
SPARE = E * REGION
SPARE_TILES = TILES - 2 * TOKENS // P
XG_ROWS = SPARE + SPARE_TILES * P
TQ = P * 2

BE2, BS2 = 0, E * C
BPROJ = BS2 + C
NBIAS = BPROJ + C

SLOTS = 8
LOOPED = (8, 136)


class Names:
    pass


class At:

    def __init__(self, k, q=0, n=4):
        self.k, self.q, self.n = k, q, n

    def __add__(self, d):
        return At(self.k + d, self.q, self.n)

    def times(self, m, d=0):
        if isinstance(self.q, int):
            return m * (self.n * self.q + self.k) + d
        return self.q * (m * self.n) + (m * self.k + d)

    def slot(self, n):
        return self.k % n

    def turn(self, n, m, d=0):
        if isinstance(self.q, int):
            return m * ((self.n * self.q + self.k) // n) + d
        return self.q * (m * (self.n // n)) + (m * (self.k // n) + d)


def wait(eng, sem, count):
    if not isinstance(count, int) or count > 0:
        eng.wait_ge(sem, count)


def apart(eng, passed):
    eng.sem_inc(passed, 1)


class Chain:

    def __init__(self, eng, sem, base=0, passed=None):
        self.eng, self.sem, self.base, self.n, self.passed = eng, sem, base, 0, passed

    def did(self, ins):
        self.n += 1
        ins.then_inc(self.sem, 1)

    def settle(self):
        self.eng.wait_ge(self.sem, self.base + self.n)
        if self.passed is not None:
            apart(self.eng, self.passed)

    def then(self, ins):
        self.did(ins)
        self.settle()


def allocate(nc, ctx):
    m = Names()

    def sb(name, shape, dt=FP32):
        return ctx.enter_context(nc.sbuf_tensor(name, shape, dt))

    m.xres = sb("xres", [P, BATCHES, NT, C])
    m.w13 = sb("w13", [P, E * KC * 2 * INTER])
    m.w2 = sb("w2", [P, E * C])
    m.b13 = sb("b13", [P, 2 * INTER])
    m.tile_b13 = sb("tile_b13", [P, 2, TILES])
    m.bias_rows = sb("bias_rows", [P, NBIAS], BF16)
    m.gate_w = sb("gate_w", [P, KC, E])
    m.gate_b = sb("gate_b", [P, E])
    m.ws1 = sb("ws1", [P, KC, SHARED])
    m.ws3 = sb("ws3", [P, KC, SHARED])
    m.ws2 = sb("ws2", [P, KC, C])
    m.bs1 = sb("bs1", [P, KC])
    m.bs3 = sb("bs3", [P, KC])
    m.w_qkv = sb("w_qkv", [P, KC, 3 * C])
    m.w_proj = sb("w_proj", [P, KC, C])
    m.ident = sb("ident", [P, P])
    m.ones3 = sb("ones3", [P, P], BF16)
    m.ones_b = sb("ones_b", [P, P], BF16)
    m.before = sb("before", [P, P], BF16)
    m.rev = sb("rev", [P, E])
    m.earlier = sb("earlier", [P, GROUPS, GROUPS])
    m.region0 = sb("region0", [P, E])
    m.part = sb("part", [P, 1])
    m.tile_no = sb("tile_no", [P, 2])
    m.head_mask = sb("head_mask", [P, P])
    m.head_of = sb("head_of", [P, CH])
    m.minus_half = sb("minus_half", [P, NT])
    m.pad = sb("pad", [P, ROW])
    m.rows = sb("rows", [P, 2 * NT * ROW])
    m.xnT = sb("xnT", [P, KC, SEQ])
    m.work = sb("work", [P, 4 * HALF])
    m.stat = sb("stat", [P, NT, 6])
    m.mv = sb("mv", [P, NT, 2])
    m.ve = sb("ve", [P, NT])
    m.rstd = sb("rstd", [P, NT])
    m.mr = sb("mr", [P, NT])
    m.nmr = sb("nmr", [P, NT])
    m.mx = sb("mx", [P, NT])
    m.sm = sb("sm", [P, NT])
    m.rs = sb("rs", [P, NT])
    m.m1 = sb("m1", [P, NT])
    m.rr = sb("rr", [P, 2, NT])
    m.m2 = sb("m2", [P, NT])
    m.tok = sb("tok", [P, NT])
    m.sh = sb("sh", [P, NT, E])
    m.ex = sb("ex", [P, NT, E])
    m.pr = sb("pr", [P, NT, E])
    m.sc = sb("sc", [P, NT, E])
    m.ms = sb("ms", [P, NT, E])
    m.e1 = sb("e1", [P, NT, E])
    m.ms2 = sb("ms2", [P, NT, E])
    m.pos = sb("pos", [P, NT, E])
    m.chosen = sb("chosen", [P, 2, NT, E])
    m.prod = sb("prod", [P, 2, NT, E])
    m.hi = sb("hi", [P, NT * GROUPS, 2])
    m.lo = sb("lo", [P, NT * GROUPS, 2])
    m.t1 = sb("t1", [P, NT * GROUPS, 1])
    m.mn = sb("mn", [P, NT * GROUPS, 1])
    m.ml = sb("ml", [P, NT * GROUPS, 1])
    m.t2 = sb("t2", [P, NT * GROUPS, 1])
    m.gs = sb("gs", [P, NT * GROUPS, 1])
    m.gt = sb("gt", [P, NT, GROUPS, GROUPS])
    m.eq = sb("eq", [P, NT, GROUPS, GROUPS])
    m.rk = sb("rk", [P, NT, GROUPS])
    m.cap = sb("cap", [P, NT * GROUPS])
    m.weight = sb("weight", [P, 2, NT])
    m.slot_f = sb("slot_f", [P, 2, NT])
    m.slots = sb("slots", [P, 2, 2, NT], U32)
    m.sel = sb("sel", [P, NT + 1, E], BF16)
    m.carry = sb("carry", [P, E])
    m.ci = sb("ci", [P, E], I32)
    m.cs = sb("cs", [P, E], I32)
    m.nt = sb("nt", [P, E])
    m.delta = sb("delta", [P, E])
    m.inc_a = sb("inc_a", [P, E])
    m.inc_b = sb("inc_b", [P, E])
    m.past = sb("past", [P, 2, E])
    m.past_d = sb("past_d", [P, 2, E])
    m.tabf = sb("tabf", [P, 4])
    m.tabr = sb("tabr", [P, 2])
    m.first = sb("first", [P, 2])
    m.pad_to = sb("pad_to", [P, E], I32)
    m.expert_of = sb("expert_of", [P, TILES])
    m.is_expert = sb("is_expert", [P, TILES])
    m.rf = sb("rf", [P, SLOTS, 2])
    m.rw0 = sb("rw0", [P, SLOTS])
    m.rw = sb("rw", [P, SLOTS])
    m.rdest = sb("rdest", [P, SLOTS], U32)
    m.xn = sb("xn", [P, NT, C])
    m.k_sb = sb("k_sb", [P, 2, C])
    m.v_sb = sb("v_sb", [P, 2, KC, P + 1])
    m.mix = sb("mix", [P, KC, P + CH])
    m.den = sb("den", [P, 2, KC, CH])
    m.z = sb("z", [P, 2, KC, CH])
    m.o_sb = sb("o_sb", [P, 2, C])
    m.oT = sb("oT", [P, 2, C])
    m.bank = [ctx.enter_context(nc.psum_tensor(f"bank{i}", [P, 512], FP32)) for i in range(8)]
    m.xs = [m.rows[:, h * NT * ROW:(h + 1) * NT * ROW].rearrange("p (i r) -> p i r", i=NT) for h in range(2)]
    m.yl = m.rows[:, 0:2 * NT * C].rearrange("p (k n) -> p k n", k=2)
    m.yl2 = m.w13[:, 0:2 * NT * C].rearrange("p (k n) -> p k n", k=2)

    def part(at, n, width):
        return m.rows[:, at:at + n * width].rearrange("p (n w) -> p n w", n=n)

    m.rin = part(0, SLOTS, ROW)
    m.rT = part(SLOTS * ROW, 2, C)
    m.rsilu = part(SLOTS * ROW + 2 * C, 2, P)
    m.rgT = part(SLOTS * ROW + 2 * C + 2 * P, 2, P)
    m.rw13 = part(SLOTS * ROW + 2 * C + 4 * P, 2, KC * C)
    m.ry = m.xn
    m.table = m.xnT[0:1, 0, 0:2 * TQ].bitcast(I32)
    m.gT = m.work[:, :].rearrange("p (g m n) -> p g m n", g=2, m=2)
    m.silu = sb("silu", [P, 2, HALF])
    m.qT = m.work[:, :].rearrange("p (m n) -> p m n", m=2)
    return m


def setup_stage(nc, m, d, sem):
    m.passed = sem("waits_passed")
    made, loaded, split, bounced, zeroed = (sem(n) for n in (
        "setup_pool_steps", "bias_loaded", "bias_split", "bias_bounced", "rows_zeroed"))
    chain_s = sem("setup_dve_steps")
    m.bias_placed, m.x_in, m.weights_in = sem("bias_placed"), sem("x_in"), sem("ffn_weights_in")
    m.loads = [(m.gate_w[:], d.gate_w), (m.gate_b[:], d.gate_b), (m.ws1[:], d.ws1), (m.ws3[:], d.ws3),
               (m.ws2[:], d.ws2), (m.bs1[:], d.bs1), (m.bs3[:], d.bs3)]
    nb = NBIAS // P
    bias_f, bias_r = m.xn[:, 0, 0:nb], m.xn[:, 1, 0:nb]
    parts = m.xn[:, 2, :].bitcast(BF16)[:, 0:3 * nb].rearrange("p (k n) -> p k n", k=3)

    with nc.Block() as block:
        @block.sync
        def _(sp):
            sp.dma_start(bias_f, d.biases.rearrange("(p f) -> p f", p=P)).then_inc(loaded, 16)
            sp.wait_ge(split, 3)
            sp.dma_start(d.bias_parts.rearrange("k (p f) -> p k f", p=P), parts).then_inc(bounced, 16)
            sp.wait_ge(bounced, 16)
            sp.wait_ge(zeroed, 1)
            sp.dma_start(m.bias_rows[0:3, :], d.bias_parts).then_inc(m.bias_placed, 16)

        @block.scalar
        def _(act):
            act.dma_start(m.xres[:, 0, :, :].rearrange("p j c -> p (j c)"),
                          d.x.rearrange("b (p j) c -> b p (j c)", p=P)[0]).then_inc(m.x_in, 16)
            for dst, src in m.loads:
                act.dma_start(dst, src).then_inc(m.weights_in, 16)

        @block.vector
        def _(dve):
            ch = Chain(dve, chain_s)
            nc.vector.memset(m.bias_rows[:, :].bitcast(U32), 0).then_inc(zeroed, 1)
            dve.wait_ge(loaded, 16)
            nc.vector.tensor_copy(parts[:, 0], bias_f).then_inc(split, 1)
            dve.wait_ge(split, 1)
            ch.then(nc.vector.tensor_tensor(bias_r, bias_f, parts[:, 0], ALU.subtract))
            nc.vector.tensor_copy(parts[:, 1], bias_r).then_inc(split, 1)
            dve.wait_ge(split, 2)
            ch.then(nc.vector.tensor_tensor(bias_f, bias_r, parts[:, 1], ALU.subtract))
            nc.vector.tensor_copy(parts[:, 2], bias_f).then_inc(split, 1)
            ch.did(nc.vector.memset(m.ones_b[:], 1.0))
            ch.then(nc.vector.memset(m.sel[:], 0.0))

        @block.gpsimd
        def _(pool):
            ch = Chain(pool, made)
            small = dict(allow_small_or_imprecise_dtypes=True)
            ch.did(nc.gpsimd.memset(m.ident[:], 0.0))
            ch.did(nc.gpsimd.memset(m.ones3[:], 0.0))
            ch.did(nc.gpsimd.memset(m.before[:], 0.0))
            ch.did(nc.gpsimd.memset(m.earlier[:], 0.0))
            ch.did(nc.gpsimd.memset(m.head_mask[:], 1.0))
            ch.did(nc.gpsimd.memset(m.minus_half[:], -0.5))
            ch.did(nc.gpsimd.memset(m.head_of[:], 1.0))
            ch.did(nc.gpsimd.memset(m.pad[:], 0.0))
            ch.did(nc.gpsimd.iota(m.rev[:], [[-1, E]], base=E, channel_multiplier=0, **small))
            ch.did(nc.gpsimd.iota(m.region0[:], [[REGION, E]], base=0, channel_multiplier=0, **small))
            ch.did(nc.gpsimd.iota(m.part[:], [[1, 1]], base=0, channel_multiplier=1, **small))
            ch.did(nc.gpsimd.iota(m.tile_no[:], [[P, 2]], base=0, channel_multiplier=1, **small))
            ch.settle()
            ch.did(nc.gpsimd.affine_select(out=m.ident[:], in_=m.ident[:], compare_op=ALU.not_equal, fill=1.0,
                                           base=0, pattern=[[-1, P]], channel_multiplier=1))
            ch.did(nc.gpsimd.affine_select(out=m.ones3[:], in_=m.ones3[:], compare_op=ALU.is_ge, fill=1.0,
                                           base=-3, pattern=[[0, P]], channel_multiplier=1))
            ch.did(nc.gpsimd.affine_select(out=m.before[:], in_=m.before[:], compare_op=ALU.is_ge, fill=1.0,
                                           base=0, pattern=[[-1, P]], channel_multiplier=1))
            ch.did(nc.gpsimd.affine_select(out=m.earlier[:], in_=m.earlier[:], compare_op=ALU.is_ge, fill=1.0,
                                           base=0, pattern=[[-1, GROUPS], [1, GROUPS]], channel_multiplier=0))
            hm = m.head_mask[:].rearrange("p (h d) -> p h d", d=HD)
            ch.did(nc.gpsimd.affine_select(out=hm, in_=hm, compare_op=ALU.is_ge, fill=0.0, base=0,
                                           pattern=[[-HD, CH], [0, HD]], channel_multiplier=1))
            ch.did(nc.gpsimd.affine_select(out=m.head_of[:], in_=m.head_of[:], compare_op=ALU.is_ge, fill=0.0,
                                           base=0, pattern=[[-HD, CH]], channel_multiplier=1))
            ch.did(nc.gpsimd.memset(m.pad[:, C:C + 1], float(2 * TOKENS)))
            ch.did(nc.gpsimd.memset(m.pad[:, C + 1:C + 3], -1.0))
            ch.settle()
            ch.did(nc.gpsimd.affine_select(out=hm, in_=hm, compare_op=ALU.is_ge, fill=0.0, base=HD - 1,
                                           pattern=[[HD, CH], [0, HD]], channel_multiplier=-1))
            ch.did(nc.gpsimd.affine_select(out=m.head_of[:], in_=m.head_of[:], compare_op=ALU.is_ge, fill=0.0,
                                           base=HD - 1, pattern=[[HD, CH]], channel_multiplier=-1))
            ch.settle()


ROUTE_STEPS = 36
META_STEPS = 6


def ffn_route_stage(nc, m, d, sem, layer):
    s = Names()
    s.stats_ready = sem(f"stats_ready{layer}")
    s.rstd_ready = sem(f"rstd_ready{layer}")
    s.xn_ready = sem(f"xn_ready{layer}")
    s.xT_ready = sem(f"xT_ready{layer}")
    s.xT_copied = sem(f"xT_copied{layer}")
    s.logits_ready = sem(f"logits_ready{layer}")
    s.shift_ready = sem(f"shift_ready{layer}")
    s.exp_ready = sem(f"exp_ready{layer}")
    s.sel_ready = sem(f"sel_ready{layer}")
    s.rank_ready = sem(f"rank_ready{layer}")
    s.rank_read = sem(f"rank_read{layer}")
    s.h1_ready = sem(f"h1_ready{layer}")
    s.h3_ready = sem(f"h3_ready{layer}")
    s.silu_ready = sem(f"silu_ready{layer}")
    s.gated_ready = sem(f"gated_ready{layer}")
    s.y_ready = sem(f"y_ready{layer}")
    s.y_added = sem(f"y_added{layer}")
    s.weights_ready = sem(f"weights_ready{layer}")
    s.slots_ready = sem(f"slots_ready{layer}")
    s.pads_ready = sem(f"pads_ready{layer}")
    s.is_expert_ready = sem(f"is_expert_ready{layer}")
    s.tile_b13_ready = sem(f"tile_b13_ready{layer}")
    s.rows_ready = sem(f"rows_ready{layer}")
    s.table_ready = sem(f"table_ready{layer}")
    s.route_steps = sem(f"route_steps{layer}")
    s.meta_steps = sem(f"meta_steps{layer}")
    s.meta_written = sem(f"meta_written{layer}")
    scattered = [sem(f"scattered{layer}_{h}") for h in range(2)]
    padded = sem(f"padded{layer}")
    if layer == 0:
        x_in, weights_in, loads = m.x_in, m.weights_in, m.loads
        later_in, spare_out = sem("later_weights_in"), sem("spare_out")
    xT_ps, logits_ps, rank_ps = m.bank[0:2], m.bank[2], m.bank[3]
    h1_ps, h3_ps = m.bank[4:6], m.bank[6:8]
    y_ps = [logits_ps[:, C:2 * C], rank_ps[:, C:2 * C]]
    logits = logits_ps[:, 0:NT * E].rearrange("p (i e) -> p i e", e=E)
    ranks = rank_ps[:, 0:(NT + 1) * E].rearrange("p (i e) -> p i e", e=E)

    def batches(eng, body):
        body(At(0, n=2))
        body(At(1, n=2))
        with eng.Fori(1, BATCHES // 2 - 1) as q:
            body(At(0, q, n=2))
            body(At(1, q, n=2))
        body(At(BATCHES - 2, n=2))
        body(At(BATCHES - 1, n=2))

    def is_last(b):
        return isinstance(b.q, int) and b.k == BATCHES - 1

    with nc.Block() as block:
        later = ((m.w13[:], d.w13), (m.w2[:], d.w2), (m.w_qkv[:], d.w_qkv), (m.w_proj[:], d.w_proj),
                 (m.b13[0:E, :], d.be13))

        def load_all(sp):
            xv = d.x.rearrange("b (p j) c -> b p (j c)", p=P)
            sp.wait_ge(x_in, 16)
            with sp.Fori(1, BATCHES) as b:
                sp.dma_start(m.xres[:, bass.ds(b, 1), :, :].rearrange("p b j c -> p (b j c)"),
                             xv[bass.ds(b, 1)].rearrange("b p n -> (b p) n")).then_inc(x_in, 16)
                sp.wait_ge(x_in, b * 16 + 16)
                apart(sp, m.passed)
            for dst, src in later:
                sp.dma_start(dst, src).then_inc(later_in, 16)
            for i in range(SPARE_TILES):
                sp.dma_start(d.xg[SPARE + i * P:SPARE + (i + 1) * P, :], m.pad[:]).then_inc(spare_out, 16)
            sp.wait_ge(weights_in, 16 * len(loads))
            sp.wait_ge(later_in, 16 * len(later))
            sp.wait_ge(spare_out, 16 * SPARE_TILES)

        @block.sync
        def _(sp):
            if layer == 0:
                load_all(sp)
            sp.wait_ge(s.pads_ready, 1)
            _, starts = nc.values_load_multi_w_load_instructions(
                m.pad_to[0:1, :], engines=(sp.engine,), min_val=0, max_val=SPARE - P,
                skip_runtime_bounds_check_because="a region holds a row for every token and a tile more")
            for start in starts:
                sp.dma_start(d.xg[bass.ds(start, P), :], m.pad[:]).then_inc(padded, 16)
            sp.wait_ge(padded, 16 * E)

        @block.tensor
        def _(pe):
            def transpose(b, g):
                pe.wait_ge(s.xn_ready, b.times(1, 1))
                for c in range(KC):
                    n = g * KC + c
                    wait(pe, s.xT_copied, b.times(4, n - 1))
                    for j in range(4):
                        last = nc.tensor.transpose(xT_ps[n % 2][:, j * P:(j + 1) * P],
                                                   m.xs[b.slot(2)][:, 4 * g + j, c * P:(c + 1) * P], m.ident[:])
                    last.then_inc(s.xT_ready, 1)

            def gate(b):
                pe.wait_ge(s.xT_copied, b.times(4, 4))
                wait(pe, s.y_added, b.times(NT, -1))
                for i in range(NT):
                    for c in range(KC):
                        last = nc.tensor.matmul(logits_ps[:, i * E:(i + 1) * E], m.xnT[:, c, i * P:(i + 1) * P],
                                                m.gate_w[:, c, :], start=c == 0, stop=c == KC - 1)
                last.then_inc(s.logits_ready, 1)

            def up(b, u):
                g, mi = divmod(u, 2)
                wait(pe, s.gated_ready, b.times(4, u - 1))
                for ws, bank, ready in ((m.ws1, h1_ps[mi], s.h1_ready), (m.ws3, h3_ps[mi], s.h3_ready)):
                    for c in range(KC):
                        last = nc.tensor.matmul(bank[:], ws[:, c, mi * P:(mi + 1) * P],
                                                m.xnT[:, c, g * HALF:(g + 1) * HALF],
                                                start=c == 0, stop=c == KC - 1)
                    last.then_inc(ready, 1)

            def down(b, g, tiles=range(NT // 2)):
                pe.wait_ge(s.gated_ready, b.times(4, 2 * g + 2))
                pe.wait_ge(s.shift_ready, b.times(1, 1))
                for t in tiles:
                    if t == 1:
                        wait(pe, s.rank_read, b.times(1, 1 if g or is_last(b) else 0))
                    wait(pe, s.y_added, b.times(NT, 4 * g + t - 1))
                    for mi in range(KC):
                        nc.tensor.matmul(y_ps[t % 2], m.gT[:, g, mi, t * P:(t + 1) * P],
                                         m.ws2[:, mi, :], start=mi == 0, stop=False)
                    nc.tensor.matmul(y_ps[t % 2], m.ones3[:], m.bias_rows[:, BS2:BS2 + C],
                                     start=False, stop=True).then_inc(s.y_ready, 1)

            def rank(b):
                pe.wait_ge(s.sel_ready, b.times(1, 1))
                wait(pe, s.rank_read, b.times(1))
                wait(pe, s.y_added, b.times(NT, 0 if is_last(b) else 4))
                nc.tensor.matmul(rank_ps[:, 0:(NT + 1) * E], m.before[:],
                                 m.sel[:].rearrange("p i e -> p (i e)"), start=True, stop=False)
                for i in range(NT):
                    last = nc.tensor.matmul(ranks[:, i + 1:, :], m.ones_b[:],
                                            m.sel[:, i:i + 1, :].to_broadcast([P, NT - i, E]),
                                            start=False, stop=i == NT - 1)
                last.then_inc(s.rank_ready, 1)

            def tables():
                pe.wait_ge(s.table_ready, 1)
                for n in range(4):
                    last = nc.tensor.matmul(xT_ps[0][:, n * P:(n + 1) * P], m.tabf[:, n:n + 1].to_broadcast([P, P]),
                                            m.ident[:], start=True, stop=True)
                last.then_inc(s.rows_ready, 1)

            if layer == 0:
                pe.wait_ge(weights_in, 16 * len(loads))
            transpose(At(0, n=2), 0)
            transpose(At(0, n=2), 1)

            def body(b):
                if layer == 0 and isinstance(b.q, int) and b.k == 0:
                    pe.wait_ge(m.bias_placed, 16)
                gate(b)
                up(b, 0)
                up(b, 1)
                up(b, 2)
                if is_last(b):
                    rank(b)
                down(b, 0)
                up(b, 3)
                if is_last(b):
                    tables()
                    down(b, 1)
                    return
                transpose(b + 1, 0)
                rank(b)
                down(b, 1, range(0, 2))
                transpose(b + 1, 1)
                down(b, 1, range(2, 4))

            batches(pe, body)

            if layer == 0:
                pe.wait_ge(later_in, 16 * len(later))
            pe.wait_ge(s.is_expert_ready, 1)
            for n in range(2):
                last = nc.tensor.matmul(xT_ps[1][:, n * TILES:(n + 1) * TILES], m.b13[0:E, n * INTER:(n + 1) * INTER],
                                        m.is_expert[0:E, :], start=True, stop=True)
            last.then_inc(s.tile_b13_ready, 1)

        @block.scalar
        def _(act):
            def normalise(b):
                act.wait_ge(s.rstd_ready, b.times(1, 1))
                for i in range(NT):
                    last = nc.scalar.activation(
                        m.xs[b.slot(2)][:, i, 0:C], m.xres[:, bass.ds(b.times(1), 1), i, :].rearrange("p b c -> p (b c)"),
                        ACT.Identity, bias=m.nmr[:, i:i + 1], scale=m.rstd[:, i:i + 1])
                last.then_inc(s.xn_ready, 1)

            def copy_xT(b):
                for n in range(4):
                    g, c = divmod(n, KC)
                    act.wait_ge(s.xT_ready, b.times(4, n + 1))
                    nc.scalar.copy(m.xnT[:, c, g * HALF:(g + 1) * HALF], xT_ps[n % 2][:]).then_inc(s.xT_copied, 1)

            def silu(b, u):
                mi = u % 2
                act.wait_ge(s.h1_ready, b.times(4, u + 1))
                nc.scalar.activation(m.silu[:, mi, :], h1_ps[mi][:], ACT.Silu,
                                     bias=m.bs1[:, mi:mi + 1]).then_inc(s.silu_ready, 1)

            def body(b):
                act.wait_ge(s.shift_ready, b.times(1, 1))
                nc.scalar.activation(m.ex[:], m.sh[:], ACT.Exp).then_inc(s.exp_ready, 1)
                silu(b, 0)
                silu(b, 1)
                silu(b, 2)
                if not is_last(b):
                    normalise(b + 1)
                silu(b, 3)
                if not is_last(b):
                    copy_xT(b + 1)

            if layer == 0:
                act.wait_ge(weights_in, 16 * len(loads))
            normalise(At(0, n=2))
            copy_xT(At(0, n=2))
            batches(act, body)

        @block.vector
        def _(dve):
            def stats(b, tiles):
                if layer == 0:
                    dve.wait_ge(x_in, b.times(16, 16))
                apart(dve, m.passed)
                for i in tiles:
                    last = nc.vector.bn_stats(
                        m.stat[:, i, :], m.xres[:, bass.ds(b.times(1), 1), i, :].rearrange("p b c -> p (b c)"))
                return last

            def aggregate():
                for i in range(NT):
                    last = nc.vector.bn_aggr(m.mv[:, i, :], m.stat[:, i, :])
                last.then_inc(s.stats_ready, 1)

            def gated(b, u):
                mi = u % 2
                dve.wait_ge(s.h3_ready, b.times(4, u + 1))
                dve.wait_ge(s.silu_ready, b.times(4, u + 1))
                wait(dve, s.y_ready, b.times(NT, 4 * (u // 2) - 4))
                nc.vector.scalar_tensor_tensor(m.gT[:, u // 2, mi, :], h3_ps[mi][:], m.bs3[:, mi:mi + 1], m.silu[:, mi, :],
                                               ALU.add, ALU.mult).then_inc(s.gated_ready, 1)

            def add_shared(b, tiles):
                for i in tiles:
                    dve.wait_ge(s.y_ready, b.times(NT, i + 1))
                    x = m.xres[:, bass.ds(b.times(1), 1), i, :].rearrange("p b c -> p (b c)")
                    nc.vector.scalar_tensor_tensor(x, y_ps[i % 2], 0.5, x, ALU.mult, ALU.add).then_inc(s.y_added, 1)

            def per_tile(ap):
                return ap.rearrange("p (i o) -> p i o", o=1).to_broadcast([P, NT, E])

            def per_expert(ap):
                return ap[:].rearrange("p (o e) -> p o e", o=1).to_broadcast([P, NT, E])

            TT, TR = nc.vector.tensor_tensor, nc.vector.tensor_reduce

            def scores(b, ch):
                dve.wait_ge(s.logits_ready, b.times(1, 1))
                ch.then(TR(m.mx[:], logits, AX.X, ALU.max))
                TT(m.sh[:], logits, per_tile(m.mx[:]), ALU.subtract).then_inc(s.shift_ready, 1)

            def groups(b, ch):
                dve.wait_ge(s.exp_ready, b.times(1, 1))
                ch.then(TR(m.sm[:], m.ex[:], AX.X, ALU.add))
                ch.then(nc.vector.reciprocal(m.rs[:], m.sm[:]))
                ch.then(TT(m.pr[:], m.ex[:], per_tile(m.rs[:]), ALU.mult))
                ch.then(TT(m.sc[:], m.pr[:], per_expert(m.gate_b), ALU.add))
                pairs = m.sc[:].rearrange("p i (g u v) -> p (i g) u v", u=2, v=2)
                ch.did(TT(m.hi[:], pairs[:, :, :, 0], pairs[:, :, :, 1], ALU.max))
                ch.then(TT(m.lo[:], pairs[:, :, :, 0], pairs[:, :, :, 1], ALU.min))
                ch.did(TT(m.t1[:], m.hi[:, :, 0:1], m.hi[:, :, 1:2], ALU.max))
                ch.did(TT(m.mn[:], m.hi[:, :, 0:1], m.hi[:, :, 1:2], ALU.min))
                ch.then(TT(m.ml[:], m.lo[:, :, 0:1], m.lo[:, :, 1:2], ALU.max))
                ch.then(TT(m.t2[:], m.mn[:], m.ml[:], ALU.max))
                ch.then(TT(m.gs[:], m.t1[:], m.t2[:], ALU.add))

            def group_ranks(ch):
                mine = m.gs[:].rearrange("p (i g) o -> p i g o", g=GROUPS).to_broadcast([P, NT, GROUPS, GROUPS])
                other = m.gs[:].rearrange("p (i g) o -> p i o g", g=GROUPS).to_broadcast([P, NT, GROUPS, GROUPS])
                earlier = m.earlier[:].rearrange("p (o g) h -> p o g h", o=1).to_broadcast([P, NT, GROUPS, GROUPS])
                ch.did(TT(m.gt[:], other, mine, ALU.is_gt))
                ch.then(TT(m.eq[:], other, mine, ALU.is_equal))
                ch.then(TT(m.eq[:], m.eq[:], earlier, ALU.mult))
                ch.then(TT(m.gt[:], m.gt[:], m.eq[:], ALU.add))

            def group_caps(ch):
                ch.then(TR(m.rk[:], m.gt[:], AX.X, ALU.add))
                ch.then(nc.vector.tensor_scalar(m.cap[:], m.rk[:].rearrange("p i g -> p (i g)"), 1.5, -2e38,
                                                ALU.subtract, ALU.mult))
                ch.then(TT(m.ms[:].rearrange("p i (g u) -> p (i g) u", u=PER_GROUP),
                           m.sc[:].rearrange("p i (g u) -> p (i g) u", u=PER_GROUP),
                           m.cap[:].rearrange("p (n o) -> p n o", o=1).to_broadcast([P, NT * GROUPS, PER_GROUP]),
                           ALU.min))

            def choose(ch, scores_ap, best, k):
                ch.then(TR(best[:], scores_ap, AX.X, ALU.max))
                ch.then(TT(m.e1[:], scores_ap, per_tile(best[:]), ALU.is_equal))
                ch.then(TT(m.e1[:], m.e1[:], per_expert(m.rev), ALU.mult))
                ch.then(TR(m.rr[:, k], m.e1[:], AX.X, ALU.max))
                ch.then(TT(m.chosen[:, k], per_expert(m.rev), per_tile(m.rr[:, k]), ALU.is_equal))

            def second(b, ch):
                ch.then(nc.vector.scalar_tensor_tensor(
                    m.ms2[:].rearrange("p i e -> p (i e)"), m.chosen[:, 0].rearrange("p i e -> p (i e)"), -3e38,
                    m.ms[:].rearrange("p i e -> p (i e)"), ALU.mult, ALU.add))
                choose(ch, m.ms2[:], m.m2, 1)
                TT(m.sel[:, 0:NT, :], m.chosen[:, 0], m.chosen[:, 1], ALU.add).then_inc(s.sel_ready, 1)

            def weights(b, ch):
                flat = m.prod[:].rearrange("p k i e -> p (k i) e")
                for k in range(2):
                    last = TT(m.prod[:, k], m.chosen[:, k], m.pr[:], ALU.mult)
                ch.then(last)
                TR(m.weight[:].rearrange("p k i -> p (k i)"), flat, AX.X, ALU.add).then_inc(s.weights_ready, 1)

            def slots(b, ch):
                dve.wait_ge(s.rank_ready, b.times(1, 1))
                dve.wait_ge(s.weights_ready, b.times(1, 1))
                ch.then(TT(m.pos[:], ranks[:, 0:NT, :], per_expert(m.carry), ALU.add))
                TT(m.carry[:], m.carry[:], ranks[:, NT, :], ALU.add).then_inc(s.rank_read, 1)
                for k in range(2):
                    last = TT(m.prod[:, k], m.chosen[:, k], m.pos[:], ALU.mult)
                ch.then(last)
                ch.then(TR(m.slot_f[:].rearrange("p k i -> p (k i)"), m.prod[:].rearrange("p k i e -> p (k i) e"),
                           AX.X, ALU.add))
                nc.vector.tensor_copy(m.slots[:, b.slot(2)], m.slot_f[:]).then_inc(s.slots_ready, 1)
                dve.wait_ge(s.rank_read, b.times(1, 1))

            def table(ch):
                nc.vector.tensor_copy(m.pad_to[:], m.carry[:]).then_inc(s.pads_ready, 1)
                ch.then(TT(m.nt[:], m.carry[:], m.region0[:], ALU.subtract))
                ch.then(nc.vector.tensor_scalar(m.ci[:], m.nt[:], float(P - 1), None, ALU.add))
                ch.then(nc.vector.tensor_scalar(m.cs[:], m.ci[:], 7, None, ALU.arith_shift_right))
                ch.then(nc.vector.tensor_copy(m.nt[:], m.cs[:]))
                ch.did(nc.vector.tensor_scalar(m.delta[:], m.nt[:], float(-P), float(REGION), ALU.mult, ALU.add))
                a, b_, step = m.nt, m.inc_a, 1
                while step < E:
                    ch.did(nc.vector.tensor_copy(b_[:, 0:step], a[:, 0:step]))
                    ch.then(TT(b_[:, step:], a[:, step:], a[:, 0:E - step], ALU.add))
                    a, b_, step = b_, (m.inc_b if b_ is m.inc_a else m.inc_a), 2 * step
                inc = a[:].rearrange("p (o e) -> p o e", o=1).to_broadcast([P, 2, E])
                no = m.tile_no[:].rearrange("p (j o) -> p j o", o=1).to_broadcast([P, 2, E])
                ch.then(TT(m.past[:], no, inc, ALU.is_ge))
                ch.did(TR(m.tabr[:], m.past[:], AX.X, ALU.add))
                ch.then(TT(m.past_d[:], m.past[:], m.delta[:].rearrange("p (o e) -> p o e", o=1).to_broadcast([P, 2, E]),
                           ALU.mult))
                ch.did(nc.vector.tensor_scalar(m.tabf[:, 0:2], m.tabr[:], float(E - 1), float(C), ALU.min, ALU.mult))
                ch.then(TR(m.first[:], m.past_d[:], AX.X, ALU.add))
                nc.vector.scalar_tensor_tensor(m.tabf[:, 2:4], m.tile_no[:], float(P), m.first[:], ALU.mult,
                                               ALU.add).then_inc(s.table_ready, 1)

            def table_rows(ch):
                dve.wait_ge(s.rows_ready, 1)
                nc.vector.tensor_copy(m.table, xT_ps[0][0:1, :])
                ch.then(nc.vector.tensor_scalar(m.expert_of[:], xT_ps[0][:, 0:TILES], 1.0 / C, None, ALU.mult))
                nc.vector.tensor_tensor(m.is_expert[:], m.expert_of[:], m.tile_no[:, 0:1].to_broadcast([P, TILES]),
                                        ALU.is_equal).then_inc(s.is_expert_ready, 1)

            def last_batch(b, ch):
                group_ranks(ch)
                group_caps(ch)
                wait(dve, s.meta_written, b.times(1))
                choose(ch, m.ms[:], m.m1, 0)
                gated(b, 1)
                second(b, ch)
                weights(b, ch)
                slots(b, ch)
                gated(b, 2)
                add_shared(b, range(0, 2))
                table(ch)
                add_shared(b, range(2, 4))
                gated(b, 3)
                add_shared(b, range(4, 7))
                table_rows(ch)
                add_shared(b, range(7, 8))

            def body(b):
                ch = Chain(dve, s.route_steps, b.times(ROUTE_STEPS, 1))
                scores(b, ch)
                groups(b, ch)
                gated(b, 0)
                if is_last(b):
                    last_batch(b, ch)
                    return
                ch.did(stats(b + 1, range(NT // 2)))
                gated(b, 1)
                ch.then(stats(b + 1, range(NT // 2, NT)))
                dve.wait_ge(s.rstd_ready, b.times(1, 1))
                apart(dve, m.passed)
                aggregate()
                gated(b, 2)
                add_shared(b, range(0, 1))
                group_ranks(ch)
                add_shared(b, range(1, 2))
                group_caps(ch)
                add_shared(b, range(2, 3))
                wait(dve, s.meta_written, b.times(1))
                choose(ch, m.ms[:], m.m1, 0)
                add_shared(b, range(3, 4))
                second(b, ch)
                weights(b, ch)
                gated(b, 3)
                slots(b, ch)
                add_shared(b, range(4, 8))
                assert ch.n == ROUTE_STEPS, ch.n

            ch = Chain(dve, s.route_steps)
            if layer == 0:
                dve.wait_ge(weights_in, 16 * len(loads))
            nc.vector.tensor_copy(m.carry[:], m.region0[:])
            ch.then(stats(At(0, n=2), range(NT)))
            aggregate()
            batches(dve, body)
            dve.wait_ge(s.tile_b13_ready, 1)
            nc.vector.tensor_copy(m.tile_b13[:].rearrange("p n t -> p (n t)"), xT_ps[1][:, 0:2 * TILES])

        @block.gpsimd
        def _(pool):
            def rstd(b, ch):
                pool.wait_ge(s.stats_ready, b.times(1, 1))
                wait(pool, scattered[b.slot(2)], b.turn(2, 16 * 2 * NT))
                apart(pool, m.passed)
                ch.then(nc.gpsimd.tensor_scalar(m.ve[:], m.mv[:, :, 1], LN_EPS, None, ALU.add))
                ch.then(nc.gpsimd.tensor_tensor(m.rstd[:], m.ve[:], m.minus_half[:], ALU.pow))
                ch.then(nc.gpsimd.tensor_tensor(m.mr[:], m.mv[:, :, 0], m.rstd[:], ALU.mult))
                nc.gpsimd.tensor_scalar(m.nmr[:], m.mr[:], -1.0, None, ALU.mult).then_inc(s.rstd_ready, 1)

            def body(b):
                ch = Chain(pool, s.meta_steps, b.times(META_STEPS, 3), m.passed)
                if not is_last(b):
                    rstd(b + 1, ch)
                xs = m.xs[b.slot(2)]
                pool.wait_ge(s.xn_ready, b.times(1, 1))
                pool.wait_ge(s.weights_ready, b.times(1, 1))
                apart(pool, m.passed)
                ch.did(nc.gpsimd.tensor_copy(xs[:, :, C:C + 1], m.tok[:].rearrange("p (i o) -> p i o", o=1)))
                ch.did(nc.gpsimd.tensor_scalar(xs[:, :, C + 1:C + 3], m.rr[:].rearrange("p k i -> p i k"),
                                               -1.0, float(E), ALU.mult, ALU.add))
                ch.then(nc.gpsimd.tensor_scalar(xs[:, :, C + 3:C + 5], m.weight[:].rearrange("p k i -> p i k"),
                                                0.5, None, ALU.mult))
                nc.gpsimd.tensor_scalar(m.tok[:], m.tok[:], float(SEQ), None, ALU.add).then_inc(s.meta_written, 1)
                pool.wait_ge(s.slots_ready, b.times(1, 1))
                apart(pool, m.passed)
                for k in range(2):
                    for i in range(NT):
                        nc.gpsimd.indirect_dma_start(
                            out=d.xg, out_offset=bass.IndirectOffsetOnAxis(ap=m.slots[:, b.slot(2), k, i:i + 1], axis=0),
                            in_=xs[:, i, :], in_offset=None).then_inc(scattered[b.slot(2)], 16)

            small = dict(allow_small_or_imprecise_dtypes=True)
            nc.gpsimd.iota(m.tok[:], [[1, NT]], base=0, channel_multiplier=NT, **small)
            rstd(At(0, n=2), Chain(pool, s.meta_steps, 0, m.passed))
            batches(pool, body)
            for h in range(2):
                pool.wait_ge(scattered[h], 16 * NT * BATCHES)


def routed_stage(nc, m, d, sem, layer):
    s = Names()
    s.rT_ready = sem(f"rT_ready{layer}")
    s.rT_copied = sem(f"rT_copied{layer}")
    s.rw13_copied = sem(f"rw13_copied{layer}")
    s.rh_ready = sem(f"rh_ready{layer}")
    s.rsilu_ready = sem(f"rsilu_ready{layer}")
    s.rgated_ready = sem(f"rgated_ready{layer}")
    s.ry_ready = sem(f"ry_ready{layer}")
    s.ry_scaled = sem(f"ry_scaled{layer}")
    s.rmeta_ready = sem(f"rmeta_ready{layer}")
    s.rmeta_steps = sem(f"rmeta_steps{layer}")
    rows_in = [sem(f"rows_in{layer}_{n}") for n in range(SLOTS)]
    rows_out = [sem(f"rows_out{layer}_{n}") for n in range(SLOTS)]
    rT_ps, h_ps, y_ps = (m.bank[2 * n:2 * n + 2] for n in range(3))

    def steps(eng, step, begin=None):
        lo, hi = LOOPED
        for t in range(-1, lo):
            step(At(t))
        with eng.Fori(0, (hi - lo) // SLOTS) as q:
            if begin:
                begin(q)
            for r in range(SLOTS):
                step(At(lo + r, q, SLOTS))
        for t in range(hi, TILES + 1):
            step(At(t))

    def experts_of(eng, first):
        values = []

        def begin(q):
            _, loaded = nc.values_load_multi_w_load_instructions(
                m.table[0:1, bass.ds(q * SLOTS + (LOOPED[0] + first), SLOTS)], engines=(eng.engine,),
                min_val=0, max_val=(E - 1) * C, skip_runtime_bounds_check_because="the table's making bounds them")
            values[:] = loaded

        def weights_at(t):
            if not isinstance(t.q, int):
                return values[t.k - (LOOPED[0] + first)]
            return eng.value_load(m.table[0:1, t.k:t.k + 1], min_val=0, max_val=(E - 1) * C)

        return begin, weights_at

    def real(t):
        return not isinstance(t.q, int) or 0 <= t.k < TILES

    with nc.Block() as block:
        @block.sync
        def _(sp):
            def load(t):
                wait(sp, s.rT_ready, t.times(1, 1 - SLOTS))
                wait(sp, s.rmeta_ready, t.times(1, 1 - SLOTS))
                apart(sp, m.passed)
                row = sp.value_load(m.table[0:1, bass.ds(t.times(1, TQ), 1)], min_val=0, max_val=XG_ROWS - P)
                sp.dma_start(m.rin[:, t.slot(SLOTS), :], d.xg[bass.ds(row, P), :]).then_inc(rows_in[t.slot(SLOTS)], 16)

            steps(sp, lambda t: load(t) if real(t) else None)

        @block.tensor
        def _(pe):
            begin, weights_at = experts_of(pe, -1)

            def step(t):
                a = t + 1
                if real(a):
                    pe.wait_ge(rows_in[a.slot(SLOTS)], a.turn(SLOTS, 16, 16))
                    wait(pe, s.rT_copied, a.times(1, -1))
                    for c in range(KC):
                        last = nc.tensor.transpose(rT_ps[a.slot(2)][:, c * P:(c + 1) * P],
                                                   m.rin[:, a.slot(SLOTS), c * P:(c + 1) * P], m.ident[:])
                    last.then_inc(s.rT_ready, 1)
                if real(t):
                    pe.wait_ge(s.rw13_copied, t.times(1, 1))
                    pe.wait_ge(s.rT_copied, t.times(1, 1))
                    wait(pe, s.rgated_ready, t.times(1, -1))
                    for n in range(2):
                        for c in range(KC):
                            last = nc.tensor.matmul(h_ps[t.slot(2)][:, n * P:(n + 1) * P],
                                                    m.rw13[:, t.slot(2), c * C + n * INTER:c * C + (n + 1) * INTER],
                                                    m.rT[:, t.slot(2), c * P:(c + 1) * P],
                                                    start=c == 0, stop=c == KC - 1)
                    last.then_inc(s.rh_ready, 1)
                y = t + -1
                if real(y):
                    e = weights_at(y)
                    pe.wait_ge(s.rgated_ready, y.times(1, 1))
                    wait(pe, s.ry_scaled, y.times(1, -1))
                    nc.tensor.matmul(y_ps[y.slot(2)][:, 0:C], m.rgT[:, y.slot(2), :],
                                     m.w2[:, bass.ds(e, C)], start=True, stop=False)
                    nc.tensor.matmul(y_ps[y.slot(2)][:, 0:C], m.ones3[:],
                                     m.bias_rows[:, BE2:BE2 + E * C][:, bass.ds(e, C)],
                                     start=False, stop=True).then_inc(s.ry_ready, 1)

            steps(pe, step, begin)

        @block.scalar
        def _(act):
            begin, weights_at = experts_of(act, 1)
            w13 = m.w13[:].rearrange("p (c n) -> p c n", c=KC)

            def step(t):
                a = t + 1
                if real(a):
                    act.wait_ge(s.rT_ready, a.times(1, 1))
                    wait(act, s.rh_ready, a.times(1, -1))
                    nc.scalar.copy(m.rT[:, a.slot(2), :], rT_ps[a.slot(2)][:, 0:C]).then_inc(s.rT_copied, 1)
                if real(a):
                    nc.scalar.copy(m.rw13[:, a.slot(2), :].rearrange("p (c n) -> p c n", c=KC),
                                   w13[:, :, bass.ds(weights_at(a), C)]).then_inc(s.rw13_copied, 1)
                if real(t):
                    act.wait_ge(s.rh_ready, t.times(1, 1))
                    wait(act, s.rgated_ready, t.times(1, -1))
                    nc.scalar.activation(m.rsilu[:, t.slot(2), :], h_ps[t.slot(2)][:, 0:P], ACT.Silu,
                                         bias=m.tile_b13[:, 0, bass.ds(t.times(1), 1)]).then_inc(s.rsilu_ready, 1)

            steps(act, step, begin)

        @block.vector
        def _(dve):
            def step(t):
                a, y = t + 1, t + -1
                n = a.slot(SLOTS)
                r, flag = m.rin[:, n, :], m.rf[:, n, :]
                ch = Chain(dve, s.rmeta_steps, a.times(2))
                if real(a):
                    dve.wait_ge(rows_in[n], a.turn(SLOTS, 16, 16))
                    wait(dve, rows_out[n], a.turn(SLOTS, 16))
                    ch.did(nc.vector.tensor_tensor(flag, r[:, C + 1:C + 3],
                                                   m.expert_of[:, bass.ds(a.times(1), 1)].to_broadcast([P, 2]),
                                                   ALU.is_equal))
                if real(t):
                    dve.wait_ge(s.rsilu_ready, t.times(1, 1))
                    wait(dve, s.ry_ready, t.times(1, -1))
                    nc.vector.scalar_tensor_tensor(
                        m.rgT[:, t.slot(2), :], h_ps[t.slot(2)][:, P:2 * P], m.tile_b13[:, 1, bass.ds(t.times(1), 1)],
                        m.rsilu[:, t.slot(2), :], ALU.add, ALU.mult).then_inc(s.rgated_ready, 1)
                if real(a):
                    ch.settle()
                    nc.vector.tensor_scalar(m.rdest[:, n:n + 1], flag[:, 1:2], float(TOKENS), r[:, C:C + 1],
                                            ALU.mult, ALU.add)
                    ch.did(nc.vector.tensor_scalar(m.rw0[:, n:n + 1], flag[:, 0:1], r[:, C + 3:C + 4], None, ALU.mult))
                if real(y):
                    dve.wait_ge(s.ry_ready, y.times(1, 1))
                    dve.wait_ge(s.rmeta_ready, y.times(1, 1))
                    wait(dve, rows_out[y.slot(SLOTS)], y.turn(SLOTS, 16))
                    nc.vector.tensor_scalar(m.ry[:, y.slot(SLOTS), :], y_ps[y.slot(2)][:, 0:C],
                                            m.rw[:, y.slot(SLOTS):y.slot(SLOTS) + 1], None,
                                            ALU.mult).then_inc(s.ry_scaled, 1)
                if real(a):
                    ch.settle()
                    nc.vector.scalar_tensor_tensor(m.rw[:, n:n + 1], flag[:, 1:2], r[:, C + 4:C + 5],
                                                   m.rw0[:, n:n + 1], ALU.mult, ALU.add).then_inc(s.rmeta_ready, 1)

            steps(dve, step)

        @block.gpsimd
        def _(pool):
            def scatter(y):
                pool.wait_ge(s.ry_scaled, y.times(1, 1))
                pool.wait_ge(s.rmeta_ready, y.times(1, 1))
                apart(pool, m.passed)
                nc.gpsimd.indirect_dma_start(
                    out=d.yt, out_offset=bass.IndirectOffsetOnAxis(ap=m.rdest[:, y.slot(SLOTS):y.slot(SLOTS) + 1], axis=0),
                    in_=m.ry[:, y.slot(SLOTS), :], in_offset=None,
                    bounds_check=2 * TOKENS - 1, oob_is_err=False).then_inc(rows_out[y.slot(SLOTS)], 16)

            steps(pool, lambda t: scatter(t + -1) if real(t + -1) else None)
            for n in range(SLOTS):
                pool.wait_ge(rows_out[n], 16 * (TILES // SLOTS))


def attention_stage(nc, m, d, sem):
    s = Names()
    s.routed_in = sem("routed_in")
    s.combined = sem("combined")
    s.a_stats_ready = sem("a_stats_ready")
    s.a_rstd_ready = sem("a_rstd_ready")
    s.a_xn_ready = sem("a_xn_ready")
    s.a_xT_ready = sem("a_xT_ready")
    s.a_xT_copied = sem("a_xT_copied")
    s.kv_ready = sem("kv_ready")
    s.kv_copied = sem("kv_copied")
    s.ctx_ready = sem("ctx_ready")
    s.mixer_ready = sem("mixer_ready")
    s.q_ready = sem("q_ready")
    s.q_copied = sem("q_copied")
    s.out_ready = sem("out_ready")
    s.out_scaled = sem("out_scaled")
    s.oT_ready = sem("oT_ready")
    s.oT_copied = sem("oT_copied")
    s.proj_ready = sem("proj_ready")
    s.proj_added = sem("proj_added")
    s.a_steps = sem("a_steps")
    s.a_rstd_steps = sem("a_rstd_steps")
    s.v_ones = sem("v_ones")
    xT_ps, kv_ps, ctx_ps, q_ps = (m.bank[2 * n:2 * n + 2] for n in range(4))
    out_ps, oT_ps, proj_ps = kv_ps, ctx_ps, q_ps
    xn = m.xn
    W = P + CH

    def batches(eng, body):
        body(At(0, n=1))
        with eng.Fori(1, BATCHES - 1) as q:
            body(At(0, q, n=1))
        body(At(BATCHES - 1, n=1))

    def is_last(b):
        return isinstance(b.q, int) and b.k == BATCHES - 1

    with nc.Block() as block:
        @block.sync
        def _(sp):
            yv = d.yt.rearrange("(k b p j) c -> b p k (j c)", k=2, b=BATCHES, p=P)

            def load(b):
                wait(sp, s.combined, b.times(1))
                sp.dma_start(m.yl, yv[bass.ds(b.times(1), 1)].rearrange("b p k n -> (b p) k n")
                             ).then_inc(s.routed_in, 16)

            batches(sp, load)

        @block.tensor
        def _(pe):
            def transpose(b):
                pe.wait_ge(s.a_xn_ready, b.times(1, 1))
                for n in range(4):
                    g, c = divmod(n, KC)
                    wait(pe, s.a_xT_copied, b.times(4, n - 1))
                    for j in range(4):
                        last = nc.tensor.transpose(xT_ps[n % 2][:, j * P:(j + 1) * P],
                                                   xn[:, 4 * g + j, c * P:(c + 1) * P], m.ident[:])
                    last.then_inc(s.a_xT_ready, 1)

            def keys_values(b, i):
                wait(pe, s.kv_copied, b.times(NT, i - 1))
                wait(pe, s.out_scaled, b.times(NT))
                for c in range(KC):
                    last = nc.tensor.matmul(kv_ps[i % 2][:], m.xnT[:, c, i * P:(i + 1) * P],
                                            m.w_qkv[:, c, C:3 * C], start=c == 0, stop=c == KC - 1)
                last.then_inc(s.kv_ready, 1)

            def context(b, i):
                pe.wait_ge(s.kv_copied, b.times(NT, i + 1))
                wait(pe, s.oT_copied, b.times(NT))
                for c in range(KC):
                    last = nc.tensor.matmul(ctx_ps[c][:, 0:P + 1], m.k_sb[:, i % 2, c * P:(c + 1) * P],
                                            m.v_sb[:, i % 2, c, :], start=i == 0, stop=i == NT - 1)
                last.then_inc(s.ctx_ready, 1)

            def queries(b):
                for n in range(4):
                    g, mi = divmod(n, 2)
                    wait(pe, s.q_copied, b.times(4, n - 1))
                    wait(pe, s.proj_added, b.times(NT))
                    for c in range(KC):
                        last = nc.tensor.matmul(q_ps[n % 2][:], m.w_qkv[:, c, mi * P:(mi + 1) * P],
                                                m.xnT[:, c, g * HALF:(g + 1) * HALF],
                                                start=c == 0, stop=c == KC - 1)
                    last.then_inc(s.q_ready, 1)

            def outputs(b, i):
                wait(pe, s.out_scaled, b.times(NT, i - 1))
                for c in range(KC):
                    last = nc.tensor.matmul(out_ps[i % 2][:, c * W:(c + 1) * W], m.qT[:, c, i * P:(i + 1) * P],
                                            m.mix[:, c, :], start=True, stop=True)
                last.then_inc(s.out_ready, 1)

            def transpose_out(b, i):
                pe.wait_ge(s.out_scaled, b.times(NT, i + 1))
                wait(pe, s.oT_copied, b.times(NT, i - 1))
                for c in range(KC):
                    last = nc.tensor.transpose(oT_ps[i % 2][:, c * P:(c + 1) * P],
                                               m.o_sb[:, i % 2, c * P:(c + 1) * P], m.ident[:])
                last.then_inc(s.oT_ready, 1)

            def project(b, i):
                pe.wait_ge(s.oT_copied, b.times(NT, i + 1))
                wait(pe, s.proj_added, b.times(NT, i - 1))
                for c in range(KC):
                    nc.tensor.matmul(proj_ps[i % 2][:, 0:C], m.oT[:, i % 2, c * P:(c + 1) * P], m.w_proj[:, c, :],
                                     start=c == 0, stop=False)
                nc.tensor.matmul(proj_ps[i % 2][:, 0:C], m.ones3[:], m.bias_rows[:, BPROJ:BPROJ + C],
                                 start=False, stop=True).then_inc(s.proj_ready, 1)

            def body(b):
                pe.wait_ge(s.a_xT_copied, b.times(4, 4))
                for i in range(NT + 1):
                    if i < NT:
                        keys_values(b, i)
                    if i:
                        context(b, i - 1)
                queries(b)
                if not is_last(b):
                    transpose(b + 1)
                pe.wait_ge(s.mixer_ready, b.times(1, 1))
                pe.wait_ge(s.q_copied, b.times(4, 4))
                for i in range(NT + 2):
                    if i < NT:
                        outputs(b, i)
                    if 1 <= i <= NT:
                        transpose_out(b, i - 1)
                    if i >= 2:
                        project(b, i - 2)

            transpose(At(0, n=1))
            batches(pe, body)

        @block.scalar
        def _(act):
            def normalise(b, tiles):
                act.wait_ge(s.a_rstd_ready, b.times(1, 1))
                for i in tiles:
                    last = nc.scalar.activation(
                        xn[:, i, :], m.xres[:, bass.ds(b.times(1), 1), i, :].rearrange("p b c -> p (b c)"),
                        ACT.Identity, bias=m.nmr[:, i:i + 1], scale=m.rstd[:, i:i + 1])
                if i == NT - 1:
                    last.then_inc(s.a_xn_ready, 1)

            def copy_xT(b):
                for n in range(4):
                    g, c = divmod(n, KC)
                    act.wait_ge(s.a_xT_ready, b.times(4, n + 1))
                    nc.scalar.copy(m.xnT[:, c, g * HALF:(g + 1) * HALF], xT_ps[n % 2][:]).then_inc(s.a_xT_copied, 1)

            def body(b):
                if not is_last(b):
                    at = dict(zip(range(NT // 2 + 1, NT), (range(0, 3), range(3, 6), range(6, NT))))
                for i in range(NT):
                    act.wait_ge(s.kv_ready, b.times(NT, i + 1))
                    wait(act, s.ctx_ready, b.times(NT, i - 1))
                    nc.scalar.activation(m.k_sb[:, i % 2, :], kv_ps[i % 2][:, 0:C], ACT.Relu)
                    nc.scalar.copy(m.v_sb[:, i % 2, :, 0:P],
                                   kv_ps[i % 2][:, C:2 * C].rearrange("p (c n) -> p c n", c=KC)
                                   ).then_inc(s.kv_copied, 1)
                    if not is_last(b) and i in at:
                        normalise(b + 1, at[i])
                for n in range(4):
                    g, mi = divmod(n, 2)
                    act.wait_ge(s.q_ready, b.times(4, n + 1))
                    nc.scalar.activation(m.qT[:, mi, g * HALF:(g + 1) * HALF], q_ps[n % 2][:],
                                         ACT.Relu).then_inc(s.q_copied, 1)
                if not is_last(b):
                    copy_xT(b + 1)
                for i in range(NT):
                    act.wait_ge(s.oT_ready, b.times(NT, i + 1))
                    wait(act, s.proj_ready, b.times(NT, i - 1))
                    nc.scalar.copy(m.oT[:, i % 2, :], oT_ps[i % 2][:, 0:C]).then_inc(s.oT_copied, 1)

            act.wait_ge(s.v_ones, 1)
            normalise(At(0, n=1), range(NT))
            copy_xT(At(0, n=1))
            batches(act, body)

        @block.vector
        def _(dve):
            STEPS = 2 + 2 * NT
            TT = nc.vector.tensor_tensor

            def combine(b, ch):
                x = m.xres[:, bass.ds(b.times(1), 1), :, :].rearrange("p b i c -> p (b i c)")
                dve.wait_ge(s.routed_in, b.times(16, 16))
                ch.then(TT(x, x, m.yl[:, 0, :], ALU.add))
                TT(x, x, m.yl[:, 1, :], ALU.add).then_inc(s.combined, 1)
                dve.wait_ge(s.combined, b.times(1, 1))
                apart(dve, m.passed)
                for i in range(NT):
                    last = nc.vector.bn_stats(
                        m.stat[:, i, :], m.xres[:, bass.ds(b.times(1), 1), i, :].rearrange("p b c -> p (b c)"))
                ch.did(last)
                ch.settle()
                wait(dve, s.a_rstd_ready, b.times(1))
                apart(dve, m.passed)
                for i in range(NT):
                    last = nc.vector.bn_aggr(m.mv[:, i, :], m.stat[:, i, :])
                last.then_inc(s.a_stats_ready, 1)

            def mixer(b):
                dve.wait_ge(s.ctx_ready, b.times(NT, NT))
                for c in range(KC):
                    TT(m.mix[:, c, 0:P], ctx_ps[c][:, 0:P], m.head_mask[:], ALU.mult)
                    last = nc.vector.tensor_scalar(m.mix[:, c, P:W], m.head_of[:], ctx_ps[c][:, P:P + 1], None,
                                                   ALU.mult)
                last.then_inc(s.mixer_ready, 1)

            def scale(b, i, ch):
                dve.wait_ge(s.out_ready, b.times(NT, i + 1))
                wait(dve, s.oT_ready, b.times(NT, i - 1))
                o = out_ps[i % 2][:, 0:KC * W].rearrange("p (c w) -> p c w", c=KC)
                ch.then(nc.vector.tensor_scalar(m.den[:, i % 2], o[:, :, P:W], EPS, None, ALU.add))
                ch.then(nc.vector.reciprocal(m.z[:, i % 2], m.den[:, i % 2]))
                TT(m.o_sb[:, i % 2, :].rearrange("p (c h d) -> p c h d", c=KC, h=CH),
                   o[:, :, 0:P].rearrange("p c (h d) -> p c h d", h=CH),
                   m.z[:, i % 2].rearrange("p c (h o) -> p c h o", o=1).to_broadcast([P, KC, CH, HD]),
                   ALU.mult).then_inc(s.out_scaled, 1)

            def add(b, i):
                dve.wait_ge(s.proj_ready, b.times(NT, i + 1))
                x = m.xres[:, bass.ds(b.times(1), 1), i, :].rearrange("p b c -> p (b c)")
                TT(x, x, proj_ps[i % 2][:, 0:C], ALU.add).then_inc(s.proj_added, 1)

            nc.vector.memset(m.v_sb[:], 1.0).then_inc(s.v_ones, 1)
            combine(At(0, n=1), Chain(dve, s.a_steps))

            def body(b):
                ch = Chain(dve, s.a_steps, b.times(STEPS, 2))
                if not is_last(b):
                    combine(b + 1, ch)
                mixer(b)
                for i in range(NT + 2):
                    if i < NT:
                        scale(b, i, ch)
                    if i >= 2:
                        add(b, i - 2)

            batches(dve, body)

        @block.gpsimd
        def _(pool):
            def rstd(b):
                ch = Chain(pool, s.a_rstd_steps, b.times(3), m.passed)
                pool.wait_ge(s.a_stats_ready, b.times(1, 1))
                wait(pool, s.a_xn_ready, b.times(1))
                apart(pool, m.passed)
                ch.then(nc.gpsimd.tensor_scalar(m.ve[:], m.mv[:, :, 1], LN_EPS, None, ALU.add))
                ch.then(nc.gpsimd.tensor_tensor(m.rstd[:], m.ve[:], m.minus_half[:], ALU.pow))
                ch.then(nc.gpsimd.tensor_tensor(m.mr[:], m.mv[:, :, 0], m.rstd[:], ALU.mult))
                nc.gpsimd.tensor_scalar(m.nmr[:], m.mr[:], -1.0, None, ALU.mult).then_inc(s.a_rstd_ready, 1)

            batches(pool, rstd)


def final_stage(nc, m, d, sem):
    routed_in = [sem(f"f_routed_in{h}") for h in range(2)]
    added, stored, steps_s = sem("f_added"), sem("f_stored"), sem("f_steps")
    buf = [m.yl, m.yl2]

    def batches(eng, body):
        body(At(0, n=2))
        body(At(1, n=2))
        with eng.Fori(1, BATCHES // 2) as q:
            body(At(0, q, n=2))
            body(At(1, q, n=2))

    with nc.Block() as block:
        @block.sync
        def _(sp):
            yv = d.yt.rearrange("(k b p j) c -> b p k (j c)", k=2, b=BATCHES, p=P)

            def load(b):
                wait(sp, added, b.times(1, -1))
                sp.dma_start(buf[b.slot(2)], yv[bass.ds(b.times(1), 1)].rearrange("b p k n -> (b p) k n")
                             ).then_inc(routed_in[b.slot(2)], 16)

            batches(sp, load)

        @block.vector
        def _(dve):
            def body(b):
                x = m.xres[:, bass.ds(b.times(1), 1), :, :].rearrange("p b i c -> p (b i c)")
                y = buf[b.slot(2)]
                dve.wait_ge(routed_in[b.slot(2)], b.turn(2, 16, 16))
                Chain(dve, steps_s, b.times(1)).then(nc.vector.tensor_tensor(x, x, y[:, 0, :], ALU.add))
                nc.vector.tensor_tensor(x, x, y[:, 1, :], ALU.add).then_inc(added, 1)

            batches(dve, body)

        @block.scalar
        def _(act):
            ov = d.out.rearrange("b (p j) c -> b p (j c)", p=P)

            def store(b):
                act.wait_ge(added, b.times(1, 1))
                act.dma_start(ov[bass.ds(b.times(1), 1)].rearrange("b p n -> (b p) n"),
                              m.xres[:, bass.ds(b.times(1), 1), :, :].rearrange("p b i c -> p (b i c)")
                              ).then_inc(stored, 16)

            batches(act, store)
            act.wait_ge(stored, 16 * BATCHES)


def build(nc, drams):
    d = Names()
    d.x = drams["x"]
    d.gate_w = drams["gate_w"]
    d.gate_b = drams["gate_b"]
    d.w13 = drams["w13"]
    d.w2 = drams["w2"]
    d.ws1 = drams["ws1"]
    d.ws3 = drams["ws3"]
    d.ws2 = drams["ws2"]
    d.bs1 = drams["bs1"]
    d.bs3 = drams["bs3"]
    d.w_qkv = drams["w_qkv"]
    d.w_proj = drams["w_proj"]
    d.be13 = drams["be13"]
    d.biases = drams["biases"]
    d.out = drams["out"]
    d.xg = nc.dram_tensor("expert_rows", (XG_ROWS, ROW), FP32, kind="Internal").ap()
    d.yt = nc.dram_tensor("routed_rows", (2 * TOKENS, C), FP32, kind="Internal").ap()
    d.bias_parts = nc.dram_tensor("bias_parts", (3, NBIAS), BF16, kind="Internal").ap()
    with ExitStack() as ctx:
        m = allocate(nc, ctx)

        def sem(name):
            return ctx.enter_context(nc.semaphore(name))

        setup_stage(nc, m, d, sem)
        ffn_route_stage(nc, m, d, sem, 0)
        routed_stage(nc, m, d, sem, 0)
        attention_stage(nc, m, d, sem)
        ffn_route_stage(nc, m, d, sem, 1)
        routed_stage(nc, m, d, sem, 1)
        final_stage(nc, m, d, sem)


def kernel(**inputs):
    import concourse.bacc as _bacc
    from concourse.bass_utils import run_bass_kernel_spmd as _run

    a = {n: np.ascontiguousarray(v) for n, v in inputs.items()}
    f = "L0_ffn_"

    def chunks(w):
        return w.reshape(-1, P, w.shape[1]).transpose(1, 0, 2)

    w13 = np.concatenate([a[f + "We1"], a[f + "We3"]], axis=2)
    laid = {
        "x": a["L0_attn_x"],
        "gate_w": chunks(a[f + "gate_w"].T),
        "gate_b": np.broadcast_to(a[f + "gate_b"], (P, E)),
        "w13": w13.reshape(E, KC, P, 2 * INTER).transpose(2, 1, 0, 3).reshape(P, -1),
        "w2": a[f + "We2"].transpose(1, 0, 2).reshape(P, -1),
        "ws1": chunks(a[f + "ws1"]),
        "ws3": chunks(a[f + "ws3"]),
        "ws2": chunks(a[f + "ws2"]),
        "bs1": a[f + "bs1"].reshape(KC, P).T,
        "bs3": a[f + "bs3"].reshape(KC, P).T,
        "w_qkv": chunks(a["L0_attn_w_qkv"].T),
        "w_proj": chunks(a["L0_attn_w_proj"].T),
        "be13": np.concatenate([a[f + "be1"], a[f + "be3"]], axis=1),
        "biases": np.concatenate([a[f + "be2"].reshape(-1), a[f + "bs2"], a["L0_attn_b_proj"]]),
    }
    nc = _bacc.Bacc("TRN2", target_bir_lowering=False, num_devices=1)
    arrays = {}
    drams = {}
    for name, v in laid.items():
        v = np.ascontiguousarray(v)
        arrays[f"in_{name}"] = v
        drams[name] = nc.dram_tensor(f"in_{name}", v.shape, mybir.dt.from_np(v.dtype), kind="ExternalInput").ap()
    drams["out"] = nc.dram_tensor("out_0", (BATCHES, SEQ, C), FP32, kind="ExternalOutput").ap()
    build(nc, drams)
    r = _run(nc, [arrays], core_ids=[0])
    return r.results[0]["out_0"]
```
